# Optimizing a Trainium2 kernel written in Bass

```python
import numpy as np
import jax
import jax.numpy as jnp

def _softmax(x, axis=-1):
    return jax.nn.softmax(x, axis=axis)

def _gelu(x):
    return jax.nn.gelu(x, approximate=True)

def _silu(x):
    return jax.nn.silu(x)

def _sigmoid(x):
    return jax.nn.sigmoid(x)

def _layernorm(x, axis=-1, eps=1e-05):
    m = jnp.mean(x, axis=axis, keepdims=True)
    v = jnp.var(x, axis=axis, keepdims=True)
    return (x - m) / jnp.sqrt(v + eps)

def _scatter_add(tgt, idx, src, axis=0):
    return tgt.at[idx].add(src)

def _segment_sum(src, seg, n):
    return jax.ops.segment_sum(src, seg, n)
kernel_name = 'mk_xattn_ffn_d1_seqx_r4_1ec210'

def setup_inputs(seed: int=0):
    np.random.seed(seed)
    _w = jnp.asarray

    def _rec_inputs():
        import jax
        import jax.numpy as jnp
        _rk = jax.random.key(seed)
        x = -0.0002928 + 1 * jax.random.normal(jax.random.fold_in(_rk, 1), (4, 512, 512), jnp.float32)
        _lenS = 512 - jax.random.randint(jax.random.fold_in(_rk, 7), (4,), 0, max(1, 512 // 4) + 1, jnp.int32)
        _lenS2 = 1601 - jax.random.randint(jax.random.fold_in(_rk, 8), (4,), 0, max(1, 1601 // 4) + 1, jnp.int32)
        _ctx_512P = jax.random.normal(jax.random.fold_in(_rk, 11), (4, 16, 128), jnp.float32)
        _ctx_512c = jax.random.dirichlet(jax.random.fold_in(_rk, 511), 0.3 * jnp.ones((16,), jnp.float32), (4, 1601))
        _ctx_512t = jnp.einsum('bsk,bkd->bsd', _ctx_512c, _ctx_512P)
        _ctx_512t = _ctx_512t * jax.lax.rsqrt(jnp.mean(jnp.square(_ctx_512t)) + 1e-12) * 0.953939
        ctx_512 = 0.000227908 + 0.99994 * (_ctx_512t + 0.3 * jax.random.normal(jax.random.fold_in(_rk, 611), (4, 1601, 128), jnp.float32))
        return (x, ctx_512)
    x, ctx_512 = _rec_inputs()

    def _L0_xattn_setup():
        import jax, jax.numpy as jnp
        import numpy as np
        B, S, L = (2, 256, 256)
        DIM_Q, H, K, D_C, D_CQ, R = (512, 16, 128, 128, 384, 64)

        def _rope_tables(length, dim):
            inv = 1.0 / 10000.0 ** (jnp.arange(0, dim, 2, dtype=jnp.float32) / dim)
            f = jnp.arange(length, dtype=jnp.float32)[:, None] * inv[None, :]
            sin = jnp.repeat(jnp.sin(f), 2, axis=-1)
            cos = jnp.repeat(jnp.cos(f), 2, axis=-1)
            return (sin, cos)

        def _rotate_half(x):
            half = x.shape[-1] // 2
            return jnp.concatenate([-x[..., half:], x[..., :half]], axis=-1)

        def _apply_rope(x, sin, cos):
            return x * cos + _rotate_half(x) * sin
        key = jax.random.key(seed)
        ks = jax.random.split(key, 8)
        return {'hidden_q': jax.random.normal(ks[0], (B, S, DIM_Q), jnp.float32), 'kv_c': jax.random.normal(ks[1], (B, L, D_C), jnp.float32), 'Wq': jax.random.normal(ks[2], (H * K, DIM_Q), jnp.float32) / np.sqrt(DIM_Q).astype(np.float32), 'w_kc_q': jax.random.normal(ks[3], (H, K, D_CQ), jnp.float32) / np.sqrt(K).astype(np.float32), 'w_kc_kv': jax.random.normal(ks[4], (H, K, D_C), jnp.float32) / np.sqrt(K).astype(np.float32), 'W_qr': jax.random.normal(ks[5], (H, D_CQ, R), jnp.float32) / np.float32(np.sqrt(D_CQ) * np.sqrt(R)), 'W_kr': jax.random.normal(ks[6], (H, D_C, R), jnp.float32) / np.sqrt(D_C).astype(np.float32), 'Wo': jax.random.normal(ks[7], (DIM_Q, H * K), jnp.float32) / np.sqrt(H * K).astype(np.float32)}
    _L0_xattn_all = _L0_xattn_setup()
    _L0_xattn_in = {k: v for k, v in _L0_xattn_all.items() if k in ('Wq', 'w_kc_q', 'w_kc_kv', 'W_qr', 'W_kr', 'Wo')}
    del _L0_xattn_all

    def _L0_ffn_setup():
        import jax, jax.numpy as jnp
        import numpy as np
        TOP_K = 2
        EPS = 1e-06
        key = jax.random.key(seed)
        ks = jax.random.split(key, 5)
        B, S, D, E = (4, 512, 512, 8)
        sd = 1.0 / np.sqrt(D)
        return {'x': jax.random.normal(ks[0], (B, S, D), jnp.float32), 'router_w': jax.random.normal(ks[1], (D, E), jnp.float32) * sd, 'router_b': jnp.zeros((E,), jnp.float32), 'expert_w': jax.random.normal(ks[2], (E, D, D), jnp.float32) * sd, 'expert_b': jnp.zeros((E, D), jnp.float32), 'proj_w': jax.random.normal(ks[3], (D, D), jnp.float32) * sd, 'proj_b': jnp.zeros((D,), jnp.float32), 'norm_w': jnp.ones((D,), jnp.float32)}
    _L0_ffn_all = _L0_ffn_setup()
    _L0_ffn_in = {k: v for k, v in _L0_ffn_all.items() if k in ('router_w', 'router_b', 'expert_w', 'expert_b', 'proj_w', 'proj_b', 'norm_w')}
    del _L0_ffn_all
    return {'x': x, 'ctx_512': ctx_512, 'L0_xattn_Wq': _L0_xattn_in['Wq'], 'L0_xattn_w_kc_q': _L0_xattn_in['w_kc_q'], 'L0_xattn_w_kc_kv': _L0_xattn_in['w_kc_kv'], 'L0_xattn_W_qr': _L0_xattn_in['W_qr'], 'L0_xattn_W_kr': _L0_xattn_in['W_kr'], 'L0_xattn_Wo': _L0_xattn_in['Wo'], 'L0_ffn_router_w': _L0_ffn_in['router_w'], 'L0_ffn_router_b': _L0_ffn_in['router_b'], 'L0_ffn_expert_w': _L0_ffn_in['expert_w'], 'L0_ffn_expert_b': _L0_ffn_in['expert_b'], 'L0_ffn_proj_w': _L0_ffn_in['proj_w'], 'L0_ffn_proj_b': _L0_ffn_in['proj_b'], 'L0_ffn_norm_w': _L0_ffn_in['norm_w']}

def reference(x, ctx_512, L0_xattn_Wq, L0_xattn_w_kc_q, L0_xattn_w_kc_kv, L0_xattn_W_qr, L0_xattn_W_kr, L0_xattn_Wo, L0_ffn_router_w, L0_ffn_router_b, L0_ffn_expert_w, L0_ffn_expert_b, L0_ffn_proj_w, L0_ffn_proj_b, L0_ffn_norm_w):
    import jax
    import jax.numpy as jnp

    def _L0_xattn_ref(hidden_q, kv_c, Wq, w_kc_q, w_kc_kv, W_qr, W_kr, Wo):
        import jax, jax.numpy as jnp
        import numpy as np
        B, S, L = (2, 256, 256)
        DIM_Q, H, K, D_C, D_CQ, R = (512, 16, 128, 128, 384, 64)

        def _rope_tables(length, dim):
            inv = 1.0 / 10000.0 ** (jnp.arange(0, dim, 2, dtype=jnp.float32) / dim)
            f = jnp.arange(length, dtype=jnp.float32)[:, None] * inv[None, :]
            sin = jnp.repeat(jnp.sin(f), 2, axis=-1)
            cos = jnp.repeat(jnp.cos(f), 2, axis=-1)
            return (sin, cos)

        def _rotate_half(x):
            half = x.shape[-1] // 2
            return jnp.concatenate([-x[..., half:], x[..., :half]], axis=-1)

        def _apply_rope(x, sin, cos):
            return x * cos + _rotate_half(x) * sin
        Bv, Sv, _ = hidden_q.shape
        _, Lv, _ = kv_c.shape
        q_hk = (hidden_q @ Wq.T).reshape(Bv, Sv, H, K)
        q_big = jnp.einsum('bshk,hkq->bshq', q_hk, w_kc_q)
        sin_q, cos_q = _rope_tables(Sv, D_CQ)
        q_big = _apply_rope(q_big, sin_q[None, :, None, :], cos_q[None, :, None, :])
        sin_k, cos_k = _rope_tables(Lv, D_C)
        kv_r = _apply_rope(kv_c, sin_k[None], cos_k[None])
        q_r = jnp.einsum('bshq,hqr->bhsr', q_big, W_qr)
        k_r = jnp.einsum('bld,hdr->bhlr', kv_r, W_kr)
        scores = jnp.einsum('bhsr,bhlr->bhsl', q_r, k_r)
        attn = jax.nn.softmax(scores, axis=-1)
        ctx_c = jnp.einsum('bhsl,bld->bhsd', attn, kv_r)
        ctx_lat = jnp.einsum('bhsd,hkd->bhsk', ctx_c, w_kc_kv)
        ctx = ctx_lat.transpose(0, 2, 1, 3).reshape(Bv, Sv, H * K)
        return ctx @ Wo.T

    def _L0_ffn_ref(x, router_w, router_b, expert_w, expert_b, proj_w, proj_b, norm_w):
        import jax, jax.numpy as jnp
        import numpy as np
        TOP_K = 2
        EPS = 1e-06
        B, S, D = x.shape
        E = router_b.shape[0]
        logits = jnp.einsum('bsd,de->bse', x, router_w) + router_b
        topk_vals, topk_idx = jax.lax.top_k(logits, TOP_K)
        topk_w = jax.nn.softmax(topk_vals, axis=-1)
        full_w = jnp.sum(jax.nn.one_hot(topk_idx, E, dtype=x.dtype) * topk_w[..., None], axis=-2)
        xf = x.reshape(-1, D)
        h = jnp.einsum('td,edf->etf', xf, expert_w) + expert_b[:, None, :]
        expert_out = jax.nn.silu(h)
        combined = jnp.einsum('etf,te->tf', expert_out, full_w.reshape(-1, E)).reshape(B, S, D)
        out = jnp.einsum('bsd,df->bsf', combined, proj_w) + proj_b
        y = x + out
        rms = jnp.sqrt(jnp.mean(y * y, axis=-1, keepdims=True) + EPS)
        return norm_w * (y / rms)
    x = x + _L0_xattn_ref(_layernorm(x, axis=-1), ctx_512, L0_xattn_Wq, L0_xattn_w_kc_q, L0_xattn_w_kc_kv, L0_xattn_W_qr, L0_xattn_W_kr, L0_xattn_Wo)
    x = x + _L0_ffn_ref(_layernorm(x, axis=-1), L0_ffn_router_w, L0_ffn_router_b, L0_ffn_expert_w, L0_ffn_expert_b, L0_ffn_proj_w, L0_ffn_proj_b, L0_ffn_norm_w)
    return x

_drawn_inputs = setup_inputs


def setup_inputs(seed=0):
    import zlib

    import numpy as np

    out = dict(_drawn_inputs(seed))
    spreads = {'L0_ffn_router_b': (0.0, 0.1),
     'L0_ffn_expert_b': (0.0, 0.375),
     'L0_ffn_proj_b': (0.0, 0.1),
     'L0_ffn_norm_w': (1.0, 0.2)}
    factors = {}
    for name, (base, spread) in spreads.items():
        noise = np.random.default_rng([zlib.crc32(name.encode()), seed]).standard_normal(out[name].shape)
        drawn = base * np.exp(spread * noise) if base else spread * noise
        out[name] = jnp.asarray(drawn.astype(out[name].dtype))
    for name, factor in factors.items():
        out[name] = (out[name] * factor).astype(out[name].dtype)
    return out
```

```python
from contextlib import ExitStack

import numpy as np

import concourse.bass as bass
from concourse import mybir

F32 = mybir.dt.float32
F32R = mybir.dt.float32r
U32 = mybir.dt.uint32
ACT = mybir.ActivationFunctionType
ALU = mybir.AluOpType
AX = mybir.AxisListType

P = 128
B, S, D = 4, 512, 512
L, C = 1601, 128
H, K, CQ, R = 16, 128, 384, 64
E = 8
LT = (L + P - 1) // P
LR = L - (LT - 1) * P
ST = S // P
KD = D // P
QT = CQ // P
CH = 402
CHUNKS = [(c * CH, min(CH, L + 1 - c * CH), min(CH, L - c * CH)) for c in range(4)]
GROUPS = [range(4 * g, min(4 * g + 4, LT)) for g in range(4)]
HW = S // 2
NT = B * ST
LN_EPS, RMS_EPS = 1e-5, 1e-6
WQ = D + CQ
PF, PL = 16 * B, 8


class Place:

    def __init__(self, h, n, p):
        self.h, self.n, self.p = h, n, p

    def has(self, d):
        return self.h is None or 0 <= self.h + d < H


def heads_of(eng, b, step):
    n0 = b * H
    for h in (0, 1):
        step(Place(h, n0 + h, h % 2))
    with eng.Fori(1, H // 2 - 1) as i:
        for p in (0, 1):
            step(Place(None, n0 + i * 2 + p, p))
    for h in range(H - 2, H + 2):
        step(Place(h, n0 + h, h % 2))


def pairs(eng, step):
    for p in (0, 1):
        step(0, p, p, True)
    with eng.Fori(1, H // 2) as i:
        for p in (0, 1):
            step(i, p, i * 2 + p, False)


def build(nc, x, kv, w_first, w_fold, w_score, router_w, router_b, expert_w, expert_b, proj_w,
          proj_b, norm_w, rope_q, rope_k, iota, out):
    with ExitStack() as ctx:
        sem = lambda name: ctx.enter_context(nc.semaphore(name))
        x1_dram = nc.dram_tensor("x1_scratch", (P, NT, D), F32).ap()
        fold_g = nc.dram_tensor("g_scratch", (H, P, CQ), F32).ap()
        fold_o = nc.dram_tensor("wo_scratch", (H, P, D), F32).ap()
        folds_stored = sem("folds_stored")
        x1_stored = sem("x1_stored")
        with ExitStack() as mem:
            fold_weights(nc, mem, sem, w_fold, w_score, fold_g, fold_o, folds_stored)
        with ExitStack() as mem:
            attention(nc, mem, sem, x, kv, w_first, fold_g, fold_o, rope_q, rope_k, folds_stored,
                      x1_dram, x1_stored)
        with ExitStack() as mem:
            experts(nc, mem, sem, x1_dram, x1_stored, router_w, router_b, expert_w, expert_b,
                    proj_w, proj_b, norm_w, iota, out)


def fold_weights(nc, mem, sem, w_fold, w_score, fold_g, fold_o, folds_stored):
    sb = lambda name, shape, dt=F32: mem.enter_context(nc.sbuf_tensor(name, shape, dt))
    fold_in = [sb(f"fold_in{p}", [P, C + D]) for p in (0, 1)]
    score_in = [sb(f"score_in{p}", [R, CQ + C]) for p in (0, 1)]
    fold_out = [sb(f"fold_out{p}", [P, CQ + D]) for p in (0, 1)]
    bank = [mem.enter_context(nc.psum_tensor(f"fold_ps{i}", [P, 512], F32)) for i in range(4)]
    loaded, made_g, made_o = [sem("fold_loaded0"), sem("fold_loaded1")], sem("made_g"), sem("made_o")
    copied_g, copied_o = sem("copied_g"), sem("copied_o")

    with nc.Block() as block:

        @block.sync
        def _(sp):
            def step(i, p, n, first):
                if p == 0 and not first:
                    sp.wait_ge(made_o, i * 2)
                sp.dma_start(fold_in[p][:], w_fold[bass.ds(n, 1)].rearrange("a p n -> (a p) n")).then_inc(loaded[p], 16)
                sp.dma_start(score_in[p][:], w_score[bass.ds(n, 1)].rearrange("a p n -> (a p) n")).then_inc(loaded[p], 16)

            pairs(sp, step)

        @block.tensor
        def _(pe):
            def step(i, p, n, first):
                pe.wait_ge(loaded[p], i * 32 + 32)
                if p == 0 and not first:
                    pe.wait_ge(copied_g, i * 2)
                    pe.wait_ge(copied_o, i * 2)
                for m in range(QT):
                    mm = nc.tensor.matmul(bank[2 * p][:, m * P:(m + 1) * P], score_in[p][:, m * P:(m + 1) * P],
                                          score_in[p][:, CQ:CQ + C], start=True, stop=True)
                mm.then_inc(made_g, 1)
                nc.tensor.matmul(bank[2 * p + 1][:], fold_in[p][:, 0:C], fold_in[p][:, C:C + D],
                                 start=True, stop=True).then_inc(made_o, 1)

            pairs(pe, step)

        @block.vector
        def _(dve):
            def step(i, p, n, first):
                dve.wait_ge(made_g, n + 1)
                if p == 0 and not first:
                    dve.wait_ge(folds_stored, i * 64)
                nc.vector.tensor_copy(fold_out[p][:, 0:CQ], bank[2 * p][:, 0:CQ]).then_inc(copied_g, 1)

            pairs(dve, step)

        @block.scalar
        def _(act):
            def step(i, p, n, first):
                act.wait_ge(made_o, n + 1)
                if p == 0 and not first:
                    act.wait_ge(folds_stored, i * 64)
                nc.scalar.activation(fold_out[p][:, CQ:CQ + D], bank[2 * p + 1][:], ACT.Copy).then_inc(copied_o, 1)
                act.wait_ge(copied_o, n + 1)
                act.wait_ge(copied_g, n + 1)
                act.dma_start(fold_g[bass.ds(n, 1)].rearrange("a p n -> (a p) n"), fold_out[p][:, 0:CQ]).then_inc(folds_stored, 16)
                act.dma_start(fold_o[bass.ds(n, 1)].rearrange("a p n -> (a p) n"), fold_out[p][:, CQ:CQ + D]).then_inc(folds_stored, 16)

            pairs(act, step)


def attention(nc, mem, sem, x, kv, w_first, fold_g, fold_o, rope_q, rope_k, folds_stored, x1_dram,
              x1_stored):
    sb = lambda name, shape, dt=F32: mem.enter_context(nc.sbuf_tensor(name, shape, dt))
    pair = lambda name, shape: (sb(name + "_hi", shape, F32R), sb(name + "_lo", shape, F32R))

    kvT = pair("kvT", [P, LT * P])
    kvl = pair("kvl", [P, LT, C])
    xnT = pair("xnT", [P, KD, S])
    wq = pair("wq", [P, WQ + CQ])
    wo = pair("wo", [P, D])
    qk = pair("qk", [P, S])
    qr = pair("qr", [P, QT, S])
    qc = [pair(f"qc{p}", [P, S]) for p in (0, 1)]
    ctxT = pair("ctxT", [P, S])
    e32 = [sb(f"e32_{p}", [P, L + 1]) for p in (0, 1)]
    x1 = sb("x1", [P, ST, D])
    xn = [sb(f"xn{p}", [P, D]) for p in (0, 1)]
    kv_in = sb("kv_in", [P, LT, C])
    wq_in = sb("wq_in", [P, WQ + CQ])
    wo_in = sb("wo_in", [P, D])
    cos_q = sb("cos_q", [P, QT, S])
    sin_q = sb("sin_q", [P, QT, S])
    straight = sb("straight", [P, QT, S])
    turned_q = sb("turned_q", [P, QT, S])
    ident = sb("ident", [P, P])
    mx = sb("mx", [P, 4])
    mrow = sb("mrow", [P, 1])
    nmax = sb("nmax", [P, 2, ST])
    sums = sb("sums", [P, 2, ST, 4])
    rsum = sb("rsum", [P, 1])
    recip = sb("recip", [P, 2, ST])
    stats = sb("stats", [P, ST, 6])
    mv = sb("mv", [P, ST, 2])
    var = sb("var", [P, ST])
    std = sb("std", [P, ST])
    rstd = sb("rstd", [P, ST])
    with ExitStack() as shared:
        sh = lambda name, shape: shared.enter_context(nc.sbuf_tensor(name, shape, F32))
        cos_k, sin_k = sh("cos_k", [P, LT, C]), sh("sin_k", [P, LT, C])
        kv_r, kv_t = sh("kv_r", [P, LT, C]), sh("kv_t", [P, LT, C])
    eT = [pair(f"eT{f}", [P, LT, HW]) for f in (0, 1)]
    psum = lambda name, shape: mem.enter_context(nc.psum_tensor(name, shape, F32))
    score_bank = psum("score_bank", [P, 4, 512])
    turn_bank = [psum(f"turn_bank{i}", [P, 4, P]) for i in (0, 1)]
    ctx_bank = psum("ctx_bank", [P, S])
    item_bank = psum("item_bank", [P, 512])

    tables_in, kv_loaded, krope_in, x_in = sem("tables_in"), sem("kv_loaded"), sem("krope_in"), sem("x_in")
    wq_loaded, wo_loaded = sem("wq_loaded"), sem("wo_loaded")
    ident_zero, ident_ready, pad_ready = sem("ident_zero"), sem("ident_ready"), sem("pad_ready")
    stat_made, var_ready, eps_added, std_ready, rstd_ready, xn_ready = (sem("stat_made"), sem("var_ready"),
        sem("eps_added"), sem("std_ready"), sem("rstd_ready"), sem("xn_ready"))
    kv_mult, kv_roped, kv_hi, kv_lo = sem("kv_mult"), sem("kv_roped"), sem("kv_hi"), sem("kv_lo")
    pro_turned, pro_hi, pro_lo = sem("pro_turned"), sem("pro_hi"), sem("pro_lo")
    wq_hi, wq_lo, wo_hi, wo_lo = sem("wq_hi"), sem("wq_lo"), sem("wo_hi"), sem("wo_lo")
    scores_ready, max_part, max_row, nmax_ready = sem("scores_ready"), sem("max_part"), sem("max_row"), sem("nmax_ready")
    exp_done, sum_done, recip_done = sem("exp_done"), sem("sum_done"), sem("recip_done")
    e_turned, e_hi, e_lo = sem("e_turned"), sem("e_hi"), sem("e_lo")
    pv_done, ctx_hi, ctx_lo = sem("pv_done"), sem("ctx_hi"), sem("ctx_lo")
    qa_ready, qa_hi, qa_lo = sem("qa_ready"), sem("qa_hi"), sem("qa_lo")
    qb_ready, rope_mult, rope_sum, rope_sum2 = sem("qb_ready"), sem("rope_mult"), sem("rope_sum"), sem("rope_sum2")
    rope_hi, rope_lo, rope_lo2 = sem("rope_hi"), sem("rope_lo"), sem("rope_lo2")
    qc_ready, qc_hi, qc_lo = sem("qc_ready"), sem("qc_hi"), sem("qc_lo")
    op_ready, op_done = sem("op_ready"), sem("op_done")
    f32 = lambda ap: ap.bitcast(F32)

    with nc.Block() as block:

        @block.sync
        def _(sp):
            sp.dma_start(cos_q[:], rope_q[0]).then_inc(tables_in, 16)
            sp.dma_start(sin_q[:], rope_q[1]).then_inc(tables_in, 16)
            sp.wait_ge(pad_ready, 1)
            sp.wait_ge(folds_stored, 32 * H)
            one = lambda t, h: t[bass.ds(h, 1)].rearrange("a p n -> (a p) n")

            def load_batch(b, first):
                kv_b = kv[bass.ds(b, 1)]
                if not first:
                    sp.wait_ge(kv_mult, b * 3)
                sp.dma_start(kv_in[:, 0:LT - 1, :], kv_b[:, 0:(LT - 1) * P].rearrange("a (t p) c -> p (a t) c", p=P)).then_inc(kv_loaded, 16)
                sp.dma_start(kv_in[0:LR, LT - 1, :], kv_b[:, (LT - 1) * P:L].rearrange("a p c -> (a p) c")).then_inc(kv_loaded, 16)
                if not first:
                    sp.wait_ge(pv_done, b * 2 * H)
                sp.dma_start(cos_k[:], rope_k[0]).then_inc(krope_in, 16)
                sp.dma_start(sin_k[:], rope_k[1]).then_inc(krope_in, 16)
                if not first:
                    sp.wait_ge(x1_stored, b * 16)
                sp.dma_start(x1[:], x[bass.ds(b, 1)].rearrange("a (t p) d -> p (a t) d", p=P)).then_inc(x_in, 16)

                def load_first(h, free):
                    if free is not None:
                        sp.wait_ge(wq_lo, free)
                    sp.dma_start(wq_in[:, 0:WQ], one(w_first, h)).then_inc(wq_loaded, 16)
                    sp.dma_start(wq_in[:, WQ:WQ + CQ], one(fold_g, h)).then_inc(wq_loaded, 16)

                def load_out(h, free):
                    if free is not None:
                        sp.wait_ge(wo_lo, free)
                    sp.dma_start(wo_in[:], one(fold_o, h)).then_inc(wo_loaded, 16)

                load_first(0, None if first else b * H)
                load_first(1, b * H + 1)
                load_out(0, None if first else b * H)
                with sp.Fori(2, H) as h:
                    load_first(h, b * H + h)
                    load_out(h - 1, b * H + h - 1)
                load_out(H - 1, b * H + H - 1)

            load_batch(0, True)
            with sp.Fori(1, B) as b:
                load_batch(b, False)

        @block.gpsimd
        def _(pool):
            nc.gpsimd.memset(ident[:], 0.0).then_inc(ident_zero, 1)
            nc.gpsimd.memset(kv_in[:, LT - 1, :], 0.0).then_inc(pad_ready, 1)
            pool.wait_ge(ident_zero, 1)
            nc.gpsimd.affine_select(out=ident[:], in_=ident[:], compare_op=ALU.not_equal, fill=1.0, base=0,
                                    pattern=[[-1, P]], channel_multiplier=1).then_inc(ident_ready, 1)
            with pool.Fori(0, B * H) as n:
                for m in (0, 1):
                    pool.wait_ge(rope_mult, n * 3 + 2)
                    nc.gpsimd.tensor_tensor(straight[:, m, :], straight[:, m, :], turned_q[:, m, :], ALU.add).then_inc(rope_sum, 1)
                for m in (0, 1):
                    pool.wait_ge(rope_hi, n * 3 + m + 1)
                    nc.gpsimd.tensor_tensor(qr[1][:, m, :], straight[:, m, :], f32(qr[0][:, m, :]), ALU.subtract).then_inc(rope_lo, 1)

        @block.tensor
        def _(pe):
            def split_product(out, w, xx, first, last):
                nc.tensor.matmul(out, w[0], xx[0], start=first, stop=False)
                nc.tensor.matmul(out, w[0], xx[1], start=False, stop=False)
                return nc.tensor.matmul(out, w[1], xx[0], start=False, stop=last)

            def chain_a(n):
                pe.wait_ge(wq_lo, n + 1)
                for k in range(KD):
                    w = [t[:, k * P:(k + 1) * P] for t in wq]
                    mm = split_product(item_bank[:], w, [t[:, k, :] for t in xnT], k == 0, k == KD - 1)
                mm.then_inc(qa_ready, 1)

            def chain_b(n, m):
                if m == 0:
                    pe.wait_ge(qa_lo, n + 1)
                else:
                    pe.wait_ge(rope_mult, n * 3 + m)
                w = [t[:, D + m * P:D + (m + 1) * P] for t in wq]
                split_product(item_bank[:], w, [t[:] for t in qk], True, True).then_inc(qb_ready, 1)

            def chain_c(n):
                pe.wait_ge(rope_mult, n * 3 + 3)
                pe.wait_ge(rope_lo, n * 2 + 2)
                for m in range(QT):
                    if m == 2:
                        pe.wait_ge(rope_lo2, n + 1)
                    w = [t[:, WQ + m * P:WQ + (m + 1) * P] for t in wq]
                    mm = split_product(item_bank[:], w, [t[:, m, :] for t in qr], m == 0, m == QT - 1)
                mm.then_inc(qc_ready, 1)

            def scores(at, t, c):
                lo, width, _ = CHUNKS[c]
                if t == 0 and c == 0:
                    pe.wait_ge(qc_lo, at.n + 1)
                if t > 0 or at.h != 0:
                    pe.wait_ge(exp_done, at.n * 16 + (4 * t + c - 3))
                q = [w[:, t * P:(t + 1) * P] for w in qc[at.p]]
                split_product(score_bank[:, c, 0:width], q, [k[:, lo:lo + width] for k in kvT], True, True).then_inc(scores_ready, 1)

            def turn(n, h, t, g):
                if g == 0:
                    pe.wait_ge(exp_done, n * 16 + (4 * t + 4))
                if not (h == 0 and t == 0 and g < 2):
                    pe.wait_ge(e_lo, n * 16 + (4 * t + g - 1))
                for i, lt in enumerate(GROUPS[g]):
                    rows = min(P, L - lt * P)
                    mm = nc.tensor.transpose(turn_bank[g % 2][0:rows, i, :], e32[t % 2][:, lt * P:lt * P + rows], ident[:])
                mm.then_inc(e_turned, 1)

            def context(n, half, part, first=False):
                out = ctx_bank[:, half * HW:(half + 1) * HW]
                if part == 0:
                    pe.wait_ge(e_lo, n * 16 + (8 * half + 8))
                    if half == 0 and not first:
                        pe.wait_ge(ctx_lo, n)
                kp, ep = ((0, 0), (0, 1), (1, 0))[part]
                for lt in range(LT):
                    rows = min(P, L - lt * P)
                    mm = nc.tensor.matmul(out, kvl[kp][0:rows, lt, :], eT[half][ep][0:rows, lt, :],
                                          start=(part == 0 and lt == 0), stop=(part == 2 and lt == LT - 1))
                if part == 2:
                    mm.then_inc(pv_done, 1)

            def project(n, j, chain, first=False):
                if j == 0:
                    pe.wait_ge(wo_lo, n + 1)
                    pe.wait_ge(ctx_lo, n + 1)
                    if chain:
                        pe.wait_ge(qc_lo, n + 3)
                if not (first and j == 0):
                    pe.wait_ge(op_done, n * 4 + j)
                split_product(item_bank[:], [t[:, j * P:(j + 1) * P] for t in ctxT], [t[:] for t in wo], True, True).then_inc(op_ready, 1)

            def head(at):
                n = at.n
                for t in range(ST):
                    for c in range(4):
                        if at.has(0):
                            scores(at, t, c)
                        if t > 0 and at.has(0):
                            turn(n, at.h, t - 1, c)
                        if t == 0 and at.has(-1):
                            turn(n - 1, None, ST - 1, c)
                    if t == 0:
                        if at.has(-2):
                            project(n - 2, 3, False)
                        if at.has(-1):
                            context(n - 1, 0, 2)
                        if at.has(1):
                            if at.has(-2):
                                pe.wait_ge(op_done, n * 4 - 4)
                            chain_a(n + 1)
                    if t == 1:
                        if at.has(1):
                            chain_b(n + 1, 0)
                        if at.has(-1):
                            context(n - 1, 1, 0)
                        if at.has(1):
                            chain_b(n + 1, 1)
                        if at.has(-1):
                            context(n - 1, 1, 1)
                        if at.has(1):
                            chain_b(n + 1, 2)
                    if t == 2:
                        if at.has(-1):
                            context(n - 1, 1, 2)
                        if at.has(1):
                            chain_c(n + 1)
                    if t == 3:
                        for j in range(3):
                            if at.has(-1):
                                project(n - 1, j, at.has(1), at.h == 1)
                            if at.has(0) and j < 2:
                                context(n, 0, j, at.h == 0)

            pe.wait_ge(ident_ready, 1)
            with pe.Fori(0, B) as b:
                for g in range(8):
                    if g >= 2:
                        pe.wait_ge(pro_lo, b * 8 + (g - 1))
                    if g < 4:
                        pe.wait_ge(xn_ready, b * 4 + (g + 1))
                        for k in range(KD):
                            mm = nc.tensor.transpose(turn_bank[g % 2][:, k, :], xn[g % 2][:, k * P:(k + 1) * P], ident[:])
                    else:
                        if g == 4:
                            pe.wait_ge(kv_roped, b + 1)
                        for i, lt in enumerate(GROUPS[g - 4]):
                            mm = nc.tensor.transpose(turn_bank[g % 2][:, i, :], kv_r[:, lt, :], ident[:])
                    mm.then_inc(pro_turned, 1)
                n0 = b * H
                pe.wait_ge(pro_lo, b * 8 + 8)
                chain_a(n0)
                for m in range(QT):
                    chain_b(n0, m)
                chain_c(n0)
                pe.wait_ge(kv_lo, b + 1)
                heads_of(pe, b, head)

        @block.scalar
        def _(act):
            def hi(out, in_):
                return nc.scalar.activation(out, in_, ACT.Copy)

            def chain_hi(n, m):
                if m < 2:
                    act.wait_ge(rope_sum, n * 2 + (m + 1))
                else:
                    act.wait_ge(rope_sum2, n + 1)
                hi(qr[0][:, m, :], straight[:, m, :]).then_inc(rope_hi, 1)

            def turn_hi(n, h, t, g):
                act.wait_ge(e_turned, n * 16 + (4 * t + g + 1))
                half, k = t // 2, len(GROUPS[g])
                rows = P if g < 3 else LR
                if g == 0 and t % 2 == 0 and h != 0:
                    act.wait_ge(pv_done, n * 2 + (half - 1))
                hi(eT[half][0][0:rows, 4 * g:4 * g + k, (t % 2) * P:(t % 2 + 1) * P], turn_bank[g % 2][0:rows, 0:k, :]).then_inc(e_hi, 1)

            def head(at):
                n = at.n
                for t in range(ST):
                    for g in range(4):
                        if t > 0 and at.has(0):
                            turn_hi(n, at.h, t - 1, g)
                        if t == 0 and at.has(-1):
                            turn_hi(n - 1, None, ST - 1, g)
                    if at.has(0):
                        act.wait_ge(nmax_ready, n * 4 + (t + 1))
                        for c, (lo, _, width) in enumerate(CHUNKS):
                            nc.scalar.activation(e32[t % 2][:, lo:lo + width], score_bank[:, c, 0:width], ACT.Exp,
                                                 bias=nmax[:, at.p, t:t + 1],
                                                 accum_out=sums[:, at.p, t, c:c + 1]).then_inc(exp_done, 1)
                    if t == 0 and at.has(1):
                        act.wait_ge(qa_ready, n + 2)
                        hi(qk[0][:], item_bank[:]).then_inc(qa_hi, 1)
                    if t == 1:
                        if at.has(-1):
                            act.wait_ge(wo_loaded, n * 16)
                            if at.has(-2):
                                act.wait_ge(op_ready, n * 4 - 4)
                            hi(wo[0][:], wo_in[:]).then_inc(wo_hi, 1)
                        if at.has(1):
                            for m in range(QT):
                                chain_hi(n + 1, m)
                    if t == 2:
                        if at.has(-1):
                            act.wait_ge(pv_done, n * 2)
                            hi(ctxT[0][:], ctx_bank[:]).then_inc(ctx_hi, 1)
                        if at.has(1):
                            act.wait_ge(qc_ready, n + 2)
                            hi(qc[1 - at.p][0][:], item_bank[:]).then_inc(qc_hi, 1)
                    if t == 3 and at.has(2):
                        act.wait_ge(wq_loaded, n * 32 + 96)
                        hi(wq[0][:], wq_in[:]).then_inc(wq_hi, 1)

            with act.Fori(0, B) as b:
                n0 = b * H
                act.wait_ge(eps_added, b + 1)
                nc.scalar.activation(std[:], var[:], ACT.Sqrt).then_inc(std_ready, 1)
                act.wait_ge(wq_loaded, n0 * 32 + 32)
                hi(wq[0][:], wq_in[:]).then_inc(wq_hi, 1)
                for g in range(8):
                    act.wait_ge(pro_turned, b * 8 + (g + 1))
                    if g < 4:
                        hi(xnT[0][:, :, g * P:(g + 1) * P], turn_bank[g % 2][:]).then_inc(pro_hi, 1)
                    else:
                        k = len(GROUPS[g - 4])
                        lo = GROUPS[g - 4][0] * P
                        hi(kvT[0][:, lo:lo + k * P], turn_bank[g % 2][:, 0:k, :].rearrange("p k c -> p (k c)")).then_inc(pro_hi, 1)
                hi(kvl[0][:], kv_r[:]).then_inc(kv_hi, 1)
                act.wait_ge(qa_ready, n0 + 1)
                hi(qk[0][:], item_bank[:]).then_inc(qa_hi, 1)
                for m in range(QT):
                    chain_hi(n0, m)
                act.wait_ge(qc_ready, n0 + 1)
                hi(qc[0][0][:], item_bank[:]).then_inc(qc_hi, 1)
                act.wait_ge(wq_loaded, n0 * 32 + 64)
                hi(wq[0][:], wq_in[:]).then_inc(wq_hi, 1)
                heads_of(act, b, head)
                act.wait_ge(op_done, n0 * 4 + 4 * H)
                act.dma_start(x1_dram[:, bass.ds(b * ST, ST), :], x1[:]).then_inc(x1_stored, 16)

        @block.vector
        def _(dve):
            def low(out, full, high):
                return nc.vector.tensor_tensor(out, full, f32(high), ALU.subtract)

            def chain_rope(n, m, first=False):
                dve.wait_ge(qb_ready, n * 3 + (m + 1))
                if m == 0 and not first:
                    dve.wait_ge(rope_lo, n * 2)
                nc.vector.tensor_tensor(straight[:, m, :], item_bank[:], cos_q[:, m, :], ALU.mult)
                if m < 2:
                    nc.vector.tensor_tensor(turned_q[:, 1 - m, :], item_bank[:], sin_q[:, m, :], ALU.mult).then_inc(rope_mult, 1)
                else:
                    nc.vector.tensor_tensor(turned_q[64:P, m, :], item_bank[0:64, :], sin_q[0:64, m, :], ALU.mult)
                    nc.vector.tensor_tensor(turned_q[0:64, m, :], item_bank[64:P, :], sin_q[64:P, m, :], ALU.mult).then_inc(rope_mult, 1)
                    dve.wait_ge(rope_mult, n * 3 + 3)
                    nc.vector.tensor_tensor(straight[:, m, :], straight[:, m, :], turned_q[:, m, :], ALU.add).then_inc(rope_sum2, 1)
                    dve.wait_ge(rope_hi, n * 3 + 3)
                    low(qr[1][:, m, :], straight[:, m, :], qr[0][:, m, :]).then_inc(rope_lo2, 1)

            def turn_lo(n, t, g):
                dve.wait_ge(e_hi, n * 16 + (4 * t + g + 1))
                half, k = t // 2, len(GROUPS[g])
                rows = P if g < 3 else LR
                cols = slice((t % 2) * P, (t % 2 + 1) * P)
                low(eT[half][1][0:rows, 4 * g:4 * g + k, cols], turn_bank[g % 2][0:rows, 0:k, :],
                    eT[half][0][0:rows, 4 * g:4 * g + k, cols]).then_inc(e_lo, 1)

            def reciprocal(n, p, t):
                dve.wait_ge(exp_done, n * 16 + (4 * t + 4))
                nc.vector.tensor_reduce(rsum[:], sums[:, p, t, :], AX.X, ALU.add).then_inc(sum_done, 1)
                dve.wait_ge(sum_done, n * 4 + (t + 1))
                nc.vector.reciprocal(recip[:, p, t:t + 1], rsum[:]).then_inc(recip_done, 1)

            def add_output(n, p, j, first):
                dve.wait_ge(op_ready, n * 4 + (j + 1))
                if not first:
                    dve.wait_ge(op_done, n * 4 + (j - 3))
                nc.vector.scalar_tensor_tensor(x1[:, j, :], item_bank[:], recip[:, p, j:j + 1], x1[:, j, :],
                                               ALU.mult, ALU.add).then_inc(op_done, 1)

            def head(at):
                n = at.n
                for t in range(ST):
                    for c, (_, _, width) in enumerate(CHUNKS):
                        if at.has(0):
                            dve.wait_ge(scores_ready, n * 16 + (4 * t + c + 1))
                            nc.vector.tensor_reduce(mx[:, c:c + 1], score_bank[:, c, 0:width], AX.X, ALU.max).then_inc(max_part, 1)
                        if t > 0 and at.has(0):
                            turn_lo(n, t - 1, c)
                        if t == 0 and at.has(-1):
                            turn_lo(n - 1, ST - 1, c)
                    if at.has(0):
                        dve.wait_ge(max_part, n * 16 + (4 * t + 4))
                        nc.vector.tensor_reduce(mrow[:], mx[:], AX.X, ALU.max).then_inc(max_row, 1)
                        dve.wait_ge(max_row, n * 4 + (t + 1))
                        nc.vector.tensor_scalar(nmax[:, at.p, t:t + 1], mrow[:], -1.0, None, ALU.mult).then_inc(nmax_ready, 1)
                    if t > 0 and at.has(0):
                        reciprocal(n, at.p, t - 1)
                    if t == 0 and at.has(-1):
                        reciprocal(n - 1, 1 - at.p, ST - 1)
                    if t == 0:
                        if at.has(-2):
                            add_output(n - 2, at.p, 3, at.h == 2)
                        if at.has(1):
                            dve.wait_ge(qa_hi, n + 2)
                            low(qk[1][:], item_bank[:], qk[0][:]).then_inc(qa_lo, 1)
                    if t == 1:
                        if at.has(-1):
                            dve.wait_ge(wo_hi, n)
                            low(wo[1][:], wo_in[:], wo[0][:]).then_inc(wo_lo, 1)
                        if at.has(1):
                            for m in range(QT):
                                chain_rope(n + 1, m)
                    if t == 2:
                        if at.has(-1):
                            dve.wait_ge(ctx_hi, n)
                            low(ctxT[1][:], ctx_bank[:], ctxT[0][:]).then_inc(ctx_lo, 1)
                        if at.has(1):
                            dve.wait_ge(qc_hi, n + 2)
                            low(qc[1 - at.p][1][:], item_bank[:], qc[1 - at.p][0][:]).then_inc(qc_lo, 1)
                    if t == 3:
                        if at.has(-1):
                            for j in range(3):
                                add_output(n - 1, 1 - at.p, j, at.h == 1)
                        if at.has(2):
                            dve.wait_ge(wq_hi, n + 3)
                            low(wq[1][:], wq_in[:], wq[0][:]).then_inc(wq_lo, 1)

            dve.wait_ge(tables_in, 32)
            with dve.Fori(0, B) as b:
                n0 = b * H
                dve.wait_ge(x_in, b * 16 + 16)
                for t in range(ST):
                    nc.vector.bn_stats(stats[:, t, :], x1[:, t, :]).then_inc(stat_made, 1)
                dve.wait_ge(stat_made, b * 4 + 4)
                nc.vector.memset(rsum[:], 0.0)
                for t in range(ST):
                    nc.vector.bn_aggr(mv[:, t, :], stats[:, t, :]).then_inc(var_ready, 1)
                dve.wait_ge(var_ready, b * 4 + 4)
                nc.vector.tensor_scalar(var[:], mv[:, :, 1], LN_EPS, None, ALU.add).then_inc(eps_added, 1)
                dve.wait_ge(std_ready, b + 1)
                nc.vector.reciprocal(rstd[:], std[:]).then_inc(rstd_ready, 1)
                dve.wait_ge(rstd_ready, b + 1)

                def norm(t):
                    if t >= 2:
                        dve.wait_ge(pro_turned, b * 8 + (t - 1))
                    nc.vector.tensor_scalar(xn[t % 2][:], x1[:, t, :], mv[:, t, 0:1], rstd[:, t:t + 1],
                                            ALU.subtract, ALU.mult).then_inc(xn_ready, 1)

                norm(0)
                norm(1)
                dve.wait_ge(kv_loaded, b * 32 + 32)
                dve.wait_ge(krope_in, b * 32 + 32)
                hc = C // 2
                nc.vector.tensor_tensor(kv_t[:, :, 0:hc], kv_in[:, :, hc:C], sin_k[:, :, 0:hc], ALU.mult).then_inc(kv_mult, 1)
                nc.vector.tensor_tensor(kv_t[:, :, hc:C], kv_in[:, :, 0:hc], sin_k[:, :, hc:C], ALU.mult).then_inc(kv_mult, 1)
                nc.vector.tensor_tensor(kv_r[:], kv_in[:], cos_k[:], ALU.mult).then_inc(kv_mult, 1)
                dve.wait_ge(kv_mult, b * 3 + 3)
                nc.vector.tensor_tensor(kv_r[:], kv_r[:], kv_t[:], ALU.add).then_inc(kv_roped, 1)
                for g in range(8):
                    dve.wait_ge(pro_hi, b * 8 + (g + 1))
                    if g < 4:
                        low(xnT[1][:, :, g * P:(g + 1) * P], turn_bank[g % 2][:], xnT[0][:, :, g * P:(g + 1) * P]).then_inc(pro_lo, 1)
                        if g < 2:
                            norm(g + 2)
                        if g == 3:
                            dve.wait_ge(wq_hi, n0 + 1)
                            low(wq[1][:], wq_in[:], wq[0][:]).then_inc(wq_lo, 1)
                    else:
                        k = len(GROUPS[g - 4])
                        lo = GROUPS[g - 4][0] * P
                        low(kvT[1][:, lo:lo + k * P], turn_bank[g % 2][:, 0:k, :].rearrange("p k c -> p (k c)"),
                            kvT[0][:, lo:lo + k * P]).then_inc(pro_lo, 1)
                dve.wait_ge(kv_hi, b + 1)
                low(kvl[1][:], kv_r[:], kvl[0][:]).then_inc(kv_lo, 1)
                dve.wait_ge(qa_hi, n0 + 1)
                low(qk[1][:], item_bank[:], qk[0][:]).then_inc(qa_lo, 1)
                for m in range(QT):
                    chain_rope(n0, m, True)
                dve.wait_ge(qc_hi, n0 + 1)
                low(qc[0][1][:], item_bank[:], qc[0][0][:]).then_inc(qc_lo, 1)
                dve.wait_ge(wq_hi, n0 + 2)
                low(wq[1][:], wq_in[:], wq[0][:]).then_inc(wq_lo, 1)
                heads_of(dve, b, head)

def experts(nc, mem, sem, x1_dram, x1_stored, router_w, router_b, expert_w, expert_b, proj_w, proj_b,
            norm_w, iota, out):
    sb = lambda name, shape, dt=F32: mem.enter_context(nc.sbuf_tensor(name, shape, dt))
    pair = lambda name, shape: (sb(name + "_hi", shape, F32R), sb(name + "_lo", shape, F32R))
    ew = pair("ew", [P, E * KD, D])
    pw = pair("pw", [P, KD, D])
    rw = pair("rw", [P, KD, E])
    zT = [pair(f"zT{p}", [P, KD, P]) for p in (0, 1)]
    combT = pair("combT", [P, KD, P])
    stage = [sb(f"stage{i}", [P, 2, D]) for i in (0, 1)]
    eb, pb, nw, rb = sb("eb", [P, E, D]), sb("pb", [P, D]), sb("nw", [P, D]), sb("rb", [P, E])
    rw_in, lane, ident = sb("rw_in", [P, KD, E]), sb("lane", [P, E]), sb("ident2", [P, P])
    x_norm, x_res, z, y = sb("x_norm", [P, D]), sb("x_res", [P, D]), sb("z", [P, D]), sb("y", [P, D])
    hid = [sb(f"hid{i}", [P, D]) for i in (0, 1)]
    z_res = [sb(f"z_res{p}", [P, D]) for p in (0, 1)]
    comb = [sb(f"comb{p}", [P, D]) for p in (0, 1)]
    small = sb("small", [P, 64])
    col = lambda i, n=1: small[:, i:i + n]
    stats, mv, var, std, rstd = col(0, 6), col(6, 2), col(8), col(9), col(10)
    ss, ms, rms, rrms = col(11), col(12), col(13), col(14)
    diff, ratio, den, w1, w2, idxf = col(15), col(16), col(17), col(18), col(19), col(20, 2)
    logits, top, hot1, hot2 = col(24, 8), col(32, 8), col(40, 8), col(48, 8)
    idx = sb("idx", [P, 8], U32)
    full_w = [sb(f"full_w{p}", [P, E]) for p in (0, 1)]
    psum = lambda name, shape: mem.enter_context(nc.psum_tensor(name, shape, F32))
    hid_bank = [psum(f"hid_bank{i}", [P, D]) for i in range(4)]
    comb_bank, z_bank = psum("comb_bank", [P, KD, P]), psum("z_bank", [P, KD, P])
    proj_bank, router_bank = psum("proj_bank", [P, D]), psum("router_bank", [P, D])

    names = """small_in stage_in0 stage_in1 w_hi w_lo rw_hi rw_lo xn_in res_in res_ready id_zero id_ready
        z_stat z_mv z_var z_std z_rstd z_ready z_turned z_hi z_lo routed route_step diff_ready ratio_ready
        weights_ready hid_ready hid_added act_done comb_step comb_turned comb_hi comb_lo projected
        y_ready squared ms_ready rms_ready rrms_ready fin_ready out_ready out_stored""".split()
    s = {name: sem("x_" + name) for name in names}
    PIECES = E * KD // 2 + KD // 2
    piece = lambda t: (ew, t) if t < E * KD // 2 else (pw, t - E * KD // 2)
    tile_of = lambda n: (n // ST, n % ST)
    f32 = lambda ap: ap.bitcast(F32)

    with nc.Block() as block:

        @block.sync
        def _(sp):
            everyone = lambda v: v.rearrange("(a n) -> a n", a=1).broadcast_to([P, v.shape[0]])
            sp.dma_start(rw_in[:], router_w).then_inc(s["small_in"], 16)
            sp.dma_start(lane[:], iota).then_inc(s["small_in"], 16)
            sp.dma_start(rb[:], everyone(router_b)).then_inc(s["small_in"], 16)
            sp.dma_start(pb[:], everyone(proj_b)).then_inc(s["small_in"], 16)
            sp.dma_start(nw[:], everyone(norm_w)).then_inc(s["small_in"], 16)
            for e in range(E):
                sp.dma_start(eb[:, e, :], everyone(expert_b[e])).then_inc(s["small_in"], 16)
            x1_rows = x1_dram
            sp.wait_ge(x1_stored, 16 * B)
            sp.dma_start(x_norm[:], x1_rows[:, 0, :]).then_inc(s["xn_in"], 16)
            for t in range(PIECES):
                if t >= 2:
                    sp.wait_ge(s["w_lo"], t - 1)
                src = expert_w[t // 2, :, (t % 2) * 2:(t % 2) * 2 + 2, :] if t < E * KD // 2 else \
                    proj_w[:, (t - E * KD // 2) * 2:(t - E * KD // 2) * 2 + 2, :]
                sp.dma_start(stage[t % 2][:], src).then_inc(s[f"stage_in{t % 2}"], 16)
            with sp.Fori(1, NT) as n:
                sp.wait_ge(s["z_ready"], n)
                sp.dma_start(x_norm[:], x1_rows[:, bass.ds(n, 1)].rearrange("p a d -> p (a d)")).then_inc(s["xn_in"], 16)

        @block.gpsimd
        def _(pool):
            nc.gpsimd.memset(ident[:], 0.0).then_inc(s["id_zero"], 1)
            pool.wait_ge(s["id_zero"], 1)
            nc.gpsimd.affine_select(out=ident[:], in_=ident[:], compare_op=ALU.not_equal, fill=1.0, base=0,
                                    pattern=[[-1, P]], channel_multiplier=1).then_inc(s["id_ready"], 1)
            pool.wait_ge(s["small_in"], 16 * (5 + E))
            x1_rows = x1_dram
            out_rows = out.rearrange("b s d -> (b s) d").rearrange("(n p) d -> p n d", p=P)
            one = lambda v, n: v[:, bass.ds(n, 1)].rearrange("p a d -> p (a d)")

            def store(n):
                pool.wait_ge(s["fin_ready"], n + 1)
                pool.wait_ge(s["res_in"], n * 16 + 16)
                nc.gpsimd.tensor_tensor(y[:], y[:], x_res[:], ALU.add).then_inc(s["out_ready"], 1)
                pool.wait_ge(s["out_ready"], n + 1)
                pool.dma_start(one(out_rows, n), y[:]).then_inc(s["out_stored"], 16)

            pool.wait_ge(s["z_ready"], 1)
            nc.gpsimd.tensor_tensor(z_res[0][:], z[:], pb[:], ALU.add).then_inc(s["res_ready"], 1)
            pool.dma_start(x_res[:], x1_rows[:, 0, :]).then_inc(s["res_in"], 16)
            pool.wait_ge(s["z_ready"], 2)
            nc.gpsimd.tensor_tensor(z_res[1][:], z[:], pb[:], ALU.add).then_inc(s["res_ready"], 1)
            with pool.Fori(0, NT // 2 - 1) as i:
                for p in (0, 1):
                    n = i * 2 + p
                    store(n)
                    pool.dma_start(x_res[:], one(x1_rows, n + 1)).then_inc(s["res_in"], 16)
                    pool.wait_ge(s["z_ready"], n + 3)
                    nc.gpsimd.tensor_tensor(z_res[p][:], z[:], pb[:], ALU.add).then_inc(s["res_ready"], 1)
            store(NT - 2)
            pool.dma_start(x_res[:], x1_rows[:, NT - 1, :]).then_inc(s["res_in"], 16)
            store(NT - 1)
            pool.wait_ge(s["out_stored"], 16 * NT)

        @block.tensor
        def _(pe):
            def split_product(out_ap, w, xx, first, last):
                nc.tensor.matmul(out_ap, w[0], xx[0], start=first, stop=False)
                nc.tensor.matmul(out_ap, w[0], xx[1], start=False, stop=False)
                return nc.tensor.matmul(out_ap, w[1], xx[0], start=False, stop=last)

            def turn(bank, src, done):
                for k in range(KD):
                    mm = nc.tensor.transpose(bank[:, k, :], src[:, k * P:(k + 1) * P], ident[:])
                mm.then_inc(done, 1)

            def over_width(bank, w, x_of, done):
                for k in range(KD):
                    mm = split_product(bank, [t[:, k, :] for t in w], x_of(k), k == 0, k == KD - 1)
                mm.then_inc(done, 1)

            def turn_z(n):
                pe.wait_ge(s["z_ready"], n + 1)
                turn(z_bank, z, s["z_turned"])

            def route(n, p):
                pe.wait_ge(s["z_lo"], n + 1)
                over_width(router_bank[:, 0:E], zT[p], lambda k: [t[:, k, :] for t in rw], s["routed"])

            def tile(at):
                n, p = at.n, at.p
                for e in range(E):
                    if at.has(0):
                        if at.h == 0:
                            pe.wait_ge(s["w_lo"], 2 * e + 2)
                        if at.h != 0 or e >= 4:
                            pe.wait_ge(s["hid_added"], n * E + (e - 3))
                        over_width(hid_bank[e % 4][:], zT[p], lambda k: [t[:, e * KD + k, :] for t in ew], s["hid_ready"])
                    if e == 1 and at.has(-1):
                        pe.wait_ge(s["comb_step"], n * E)
                        turn(comb_bank, comb[1 - p], s["comb_turned"])
                    if e == 2 and at.has(1):
                        turn_z(n + 1)
                    if e == 3 and at.has(-1):
                        if at.h == 1:
                            pe.wait_ge(s["w_lo"], PIECES)
                        pe.wait_ge(s["comb_lo"], n)
                        over_width(proj_bank[:], combT, lambda k: [t[:, k, :] for t in pw], s["projected"])
                    if e == 4 and at.has(1):
                        route(n + 1, 1 - p)

            pe.wait_ge(s["id_ready"], 1)
            turn_z(0)
            pe.wait_ge(s["rw_lo"], 1)
            route(0, 0)
            heads_of(pe, 0, tile)

        @block.scalar
        def _(act):
            def hi(out_ap, in_):
                return nc.scalar.activation(out_ap, in_, ACT.Copy)

            def z_root(n):
                act.wait_ge(s["z_var"], n + 1)
                nc.scalar.activation(std, var, ACT.Sqrt).then_inc(s["z_std"], 1)

            def z_high(n, p):
                act.wait_ge(s["z_turned"], n + 1)
                hi(zT[p][0][:], z_bank[:]).then_inc(s["z_hi"], 1)

            def ratio_of(n):
                act.wait_ge(s["diff_ready"], n + 1)
                nc.scalar.activation(ratio, diff, ACT.Exp).then_inc(s["ratio_ready"], 1)

            def tile(at):
                n, p = at.n, at.p
                for e in range(E):
                    if at.has(0):
                        act.wait_ge(s["hid_added"], n * E + (e + 1))
                        nc.scalar.activation(hid[e % 2][:], hid[e % 2][:], ACT.Silu).then_inc(s["act_done"], 1)
                    if e == 0 and at.has(1):
                        z_root(n + 1)
                    if e == 1 and at.has(-1):
                        act.wait_ge(s["comb_turned"], n)
                        hi(combT[0][:], comb_bank[:]).then_inc(s["comb_hi"], 1)
                    if e == 3 and at.has(1):
                        z_high(n + 1, 1 - p)
                    if e == 4 and at.has(-1):
                        act.wait_ge(s["y_ready"], n)
                        nc.scalar.activation(proj_bank[:], y[:], ACT.Square, accum_out=ss).then_inc(s["squared"], 1)
                    if e == 5 and at.has(1):
                        ratio_of(n + 1)
                    if e == 6 and at.has(-1):
                        act.wait_ge(s["ms_ready"], n)
                        nc.scalar.activation(rms, ms, ACT.Sqrt).then_inc(s["rms_ready"], 1)

            act.wait_ge(s["small_in"], 16 * (5 + E))
            hi(rw[0][:], rw_in[:]).then_inc(s["rw_hi"], 1)
            z_root(0)
            z_high(0, 0)
            ratio_of(0)
            for t in range(PIECES):
                w, r = piece(t)
                act.wait_ge(s[f"stage_in{t % 2}"], 16 * (t // 2 + 1))
                hi(w[0][:, 2 * r:2 * r + 2, :], stage[t % 2][:]).then_inc(s["w_hi"], 1)
            heads_of(act, 0, tile)

        @block.vector
        def _(dve):
            def low(out_ap, full, high):
                return nc.vector.tensor_tensor(out_ap, full, f32(high), ALU.subtract)

            def z_stats(n):
                dve.wait_ge(s["xn_in"], n * 16 + 16)
                nc.vector.bn_stats(stats, x_norm[:]).then_inc(s["z_stat"], 1)
                dve.wait_ge(s["z_stat"], n + 1)
                nc.vector.memset(col(56), 0.0)
                nc.vector.bn_aggr(mv, stats).then_inc(s["z_mv"], 1)
                dve.wait_ge(s["z_mv"], n + 1)
                nc.vector.tensor_scalar(var, small[:, 7:8], LN_EPS, None, ALU.add).then_inc(s["z_var"], 1)

            def z_norm(n):
                dve.wait_ge(s["z_std"], n + 1)
                nc.vector.reciprocal(rstd, std).then_inc(s["z_rstd"], 1)
                dve.wait_ge(s["z_rstd"], n + 1)
                dve.wait_ge(s["z_turned"], n)
                dve.wait_ge(s["res_ready"], n)
                nc.vector.tensor_scalar(z[:], x_norm[:], small[:, 6:7], rstd, ALU.subtract, ALU.mult).then_inc(s["z_ready"], 1)

            def z_low(n, p):
                dve.wait_ge(s["z_hi"], n + 1)
                low(zT[p][1][:], z_bank[:], zT[p][0][:]).then_inc(s["z_lo"], 1)

            def pick(n):
                def step(i, ins):
                    ins.then_inc(s["route_step"], 1)
                    dve.wait_ge(s["route_step"], n * 9 + (i + 1))
                dve.wait_ge(s["routed"], n + 1)
                step(0, nc.vector.tensor_tensor(logits, router_bank[:, 0:E], rb[:], ALU.add))
                nc.vector.memset(col(57), 0.0)
                step(1, nc.vector.max(top, logits))
                nc.vector.tensor_tensor(diff, small[:, 33:34], small[:, 32:33], ALU.subtract).then_inc(s["diff_ready"], 1)
                step(2, nc.vector.max_index(idx[:], top, logits))
                step(3, nc.vector.tensor_copy(idxf, idx[:, 0:2]))
                nc.vector.tensor_scalar(hot1, lane[:], small[:, 20:21], None, ALU.is_equal)
                step(4, nc.vector.tensor_scalar(hot2, lane[:], small[:, 21:22], None, ALU.is_equal))

            def weigh(n, p):
                def step(i, ins):
                    ins.then_inc(s["route_step"], 1)
                    dve.wait_ge(s["route_step"], n * 9 + (i + 1))
                dve.wait_ge(s["ratio_ready"], n + 1)
                step(5, nc.vector.tensor_scalar(den, ratio, 1.0, None, ALU.add))
                step(6, nc.vector.reciprocal(w1, den))
                step(7, nc.vector.tensor_tensor(w2, ratio, w1, ALU.mult))
                step(8, nc.vector.tensor_scalar(hot1, hot1, w1, None, ALU.mult))
                nc.vector.scalar_tensor_tensor(full_w[p][:], hot2, w2, hot1, ALU.mult, ALU.add).then_inc(s["weights_ready"], 1)

            def combine(at, e):
                n, p = at.n, at.p
                dve.wait_ge(s["act_done"], n * E + (e + 1))
                w = full_w[p][:, e:e + 1]
                if e == 0:
                    dve.wait_ge(s["weights_ready"], n + 1)
                    nc.vector.tensor_scalar(comb[p][:], hid[0][:], w, None, ALU.mult).then_inc(s["comb_step"], 1)
                else:
                    dve.wait_ge(s["comb_step"], n * E + e)
                    nc.vector.scalar_tensor_tensor(comb[p][:], hid[e % 2][:], w, comb[p][:], ALU.mult, ALU.add).then_inc(s["comb_step"], 1)

            def tile(at):
                n, p = at.n, at.p
                for e in range(E):
                    if at.has(0):
                        dve.wait_ge(s["hid_ready"], n * E + (e + 1))
                        if at.h != 0 or e >= 2:
                            dve.wait_ge(s["comb_step"], n * E + (e - 1))
                        nc.vector.tensor_tensor(hid[e % 2][:], hid_bank[e % 4][:], eb[:, e, :], ALU.add).then_inc(s["hid_added"], 1)
                        if e >= 1:
                            combine(at, e - 1)
                    if e == 0 and at.has(1):
                        z_stats(n + 1)
                    if e == 1 and at.has(-1):
                        dve.wait_ge(s["comb_hi"], n)
                        low(combT[1][:], comb_bank[:], combT[0][:]).then_inc(s["comb_lo"], 1)
                    if e == 2 and at.has(1):
                        z_norm(n + 1)
                    if e == 3 and at.has(1):
                        z_low(n + 1, 1 - p)
                    if e == 4 and at.has(-1):
                        dve.wait_ge(s["projected"], n)
                        dve.wait_ge(s["res_ready"], n)
                        if at.has(-2):
                            dve.wait_ge(s["out_stored"], n * 16 - 16)
                        nc.vector.tensor_tensor(y[:], proj_bank[:], z_res[1 - p][:], ALU.add).then_inc(s["y_ready"], 1)
                    if e == 5 and at.has(-1):
                        dve.wait_ge(s["squared"], n)
                        nc.vector.tensor_scalar(ms, ss, 1.0 / D, RMS_EPS, ALU.mult, ALU.add).then_inc(s["ms_ready"], 1)
                    if e == 5 and at.has(1):
                        pick(n + 1)
                    if e == 6 and at.has(1):
                        weigh(n + 1, 1 - p)
                    if e == 7 and at.has(-1):
                        dve.wait_ge(s["rms_ready"], n)
                        nc.vector.reciprocal(rrms, rms).then_inc(s["rrms_ready"], 1)
                        dve.wait_ge(s["rrms_ready"], n)
                        nc.vector.scalar_tensor_tensor(y[:], y[:], rrms, nw[:], ALU.mult, ALU.mult).then_inc(s["fin_ready"], 1)
                if at.has(0):
                    combine(at, E - 1)

            dve.wait_ge(s["rw_hi"], 1)
            low(rw[1][:], rw_in[:], rw[0][:]).then_inc(s["rw_lo"], 1)
            z_stats(0)
            z_norm(0)
            z_low(0, 0)
            pick(0)
            weigh(0, 0)
            for t in range(PIECES):
                w, r = piece(t)
                dve.wait_ge(s["w_hi"], t + 1)
                low(w[1][:, 2 * r:2 * r + 2, :], stage[t % 2][:], w[0][:, 2 * r:2 * r + 2, :]).then_inc(s["w_lo"], 1)
            heads_of(dve, 0, tile)



def _rope(length, dim):
    inv = np.float32(1.0) / np.float32(10000.0) ** (np.arange(0, dim, 2, dtype=np.float32) / np.float32(dim))
    f = np.arange(length, dtype=np.float32)[:, None] * inv[None, :].astype(np.float32)
    return np.repeat(np.sin(f), 2, axis=-1), np.repeat(np.cos(f), 2, axis=-1)


def _layout(inputs):
    a = {k: np.asarray(v) for k, v in inputs.items()}
    order = np.r_[0:128, 192:320, 128:192, 320:384]
    wq = a["L0_xattn_Wq"].reshape(H, K, KD, P).transpose(0, 3, 2, 1).reshape(H, P, D)
    w_first = np.concatenate([wq, a["L0_xattn_w_kc_q"][:, :, order]], axis=2)
    wo = a["L0_xattn_Wo"].reshape(D, H, K).transpose(1, 2, 0)
    w_fold = np.concatenate([a["L0_xattn_w_kc_kv"], wo], axis=2)
    w_score = np.concatenate([a["L0_xattn_W_qr"][:, order, :].transpose(0, 2, 1),
                              a["L0_xattn_W_kr"].transpose(0, 2, 1)], axis=2)
    sin, cos = _rope(S, CQ)
    pack = lambda t: t.T.reshape(QT, P, S).transpose(1, 0, 2)
    partner = np.r_[192:320, 0:128, 320:384, 128:192]
    sign = np.r_[np.ones(128), -np.ones(128), np.ones(64), -np.ones(64)].astype(np.float32)
    rope_q = np.stack([pack(cos[:, order]), pack(sin[:, partner] * sign)])
    sin, cos = _rope(L, C)
    sin = sin * np.r_[-np.ones(C // 2), np.ones(C // 2)].astype(np.float32)
    pad = lambda t: np.concatenate([t, np.zeros((LT * P - L, C), np.float32)]).reshape(LT, P, C).transpose(1, 0, 2)
    rope_k = np.stack([pad(cos), pad(sin)])
    ew = a["L0_ffn_expert_w"].reshape(E, KD, P, D).transpose(0, 2, 1, 3)
    pw = a["L0_ffn_proj_w"].reshape(KD, P, D).transpose(1, 0, 2)
    rw = a["L0_ffn_router_w"].reshape(KD, P, E).transpose(1, 0, 2)
    iota = np.broadcast_to(np.arange(E, dtype=np.float32), (P, E))
    return {"x": a["x"], "kv": a["ctx_512"], "w_first": w_first, "w_fold": w_fold, "w_score": w_score,
            "router_w": rw, "router_b": a["L0_ffn_router_b"], "expert_w": ew, "expert_b": a["L0_ffn_expert_b"],
            "proj_w": pw, "proj_b": a["L0_ffn_proj_b"], "norm_w": a["L0_ffn_norm_w"],
            "rope_q": rope_q.astype(np.float32), "rope_k": rope_k.astype(np.float32), "iota": iota}


def kernel(**inputs):
    import concourse.bacc as _bacc
    from concourse.bass_utils import run_bass_kernel_spmd as _run

    nc = _bacc.Bacc("TRN2", target_bir_lowering=False, num_devices=1)
    arrays = {f"in_{k}": np.ascontiguousarray(v) for k, v in _layout(inputs).items()}
    args = [nc.dram_tensor(k, v.shape, mybir.dt.from_np(v.dtype), kind="ExternalInput").ap()
            for k, v in arrays.items()]
    args.append(nc.dram_tensor("out_dram", (B, S, D), F32, kind="ExternalOutput").ap())
    build(nc, *args)
    return _run(nc, [arrays], core_ids=[0]).results[0]["out_dram"]
```

```python
from contextlib import ExitStack

import numpy as np

import concourse.bass as bass
from concourse import mybir

F32 = mybir.dt.float32
F32R = mybir.dt.float32r
U32 = mybir.dt.uint32
ACT = mybir.ActivationFunctionType
ALU = mybir.AluOpType
AX = mybir.AxisListType

P = 128
B, S, D = 4, 512, 512
L, C = 1601, 128
H, K, CQ, R = 16, 128, 384, 64
E = 8
LT = (L + P - 1) // P
LR = L - (LT - 1) * P
ST = S // P
KD = D // P
QT = CQ // P
CH = 402
CHUNKS = [(c * CH, min(CH, L + 1 - c * CH), min(CH, L - c * CH)) for c in range(4)]
GROUPS = [range(4 * g, min(4 * g + 4, LT)) for g in range(4)]
HW = S // 2
NT = B * ST
LN_EPS, RMS_EPS = 1e-5, 1e-6
WQ = D + CQ
AK = 2


class Place:

    def __init__(self, h, n, p):
        self.h, self.n, self.p = h, n, p

    def has(self, d):
        return self.h is None or 0 <= self.h + d < H


def heads_of(eng, b, step):
    n0 = b * H
    for h in (0, 1):
        step(Place(h, n0 + h, h % 2))
    with eng.Fori(1, H // 2 - 1) as i:
        for p in (0, 1):
            step(Place(None, n0 + i * 2 + p, p))
    for h in range(H - 2, H + 1):
        step(Place(h, n0 + h, h % 2))


def pairs(eng, step):
    for p in (0, 1):
        step(0, p, p, True)
    with eng.Fori(1, H // 2) as i:
        for p in (0, 1):
            step(i, p, i * 2 + p, False)


def build(nc, x, kv, w_first, w_fold, w_score, router_w, router_b, expert_w, expert_b, proj_w,
          proj_b, norm_w, rope_q, rope_k, iota, out):
    with ExitStack() as ctx:
        sem = lambda name: ctx.enter_context(nc.semaphore(name))
        x1_dram = nc.dram_tensor("x1_scratch", (P, NT, D), F32).ap()
        fold_g = nc.dram_tensor("g_scratch", (H, P, CQ), F32).ap()
        fold_o = nc.dram_tensor("wo_scratch", (H, P, D), F32).ap()
        folds_stored = sem("folds_stored")
        x1_stored = sem("x1_stored")
        with ExitStack() as mem:
            fold_weights(nc, mem, sem, w_fold, w_score, fold_g, fold_o, folds_stored)
        with ExitStack() as mem:
            attention(nc, mem, sem, x, kv, w_first, fold_g, fold_o, rope_q, rope_k, folds_stored,
                      x1_dram, x1_stored)
        with ExitStack() as mem:
            experts(nc, mem, sem, x1_dram, x1_stored, router_w, router_b, expert_w, expert_b,
                    proj_w, proj_b, norm_w, iota, out)


def fold_weights(nc, mem, sem, w_fold, w_score, fold_g, fold_o, folds_stored):
    sb = lambda name, shape, dt=F32: mem.enter_context(nc.sbuf_tensor(name, shape, dt))
    fold_in = [sb(f"fold_in{p}", [P, C + D]) for p in (0, 1)]
    score_in = [sb(f"score_in{p}", [R, CQ + C]) for p in (0, 1)]
    fold_out = [sb(f"fold_out{p}", [P, CQ + D]) for p in (0, 1)]
    bank = [mem.enter_context(nc.psum_tensor(f"fold_ps{i}", [P, 512], F32)) for i in range(4)]
    loaded, made_g, made_o = [sem("fold_loaded0"), sem("fold_loaded1")], sem("made_g"), sem("made_o")
    copied_g, copied_o = sem("copied_g"), sem("copied_o")

    with nc.Block() as block:

        @block.sync
        def _(sp):
            def step(i, p, n, first):
                if p == 0 and not first:
                    sp.wait_ge(made_o, i * 2)
                sp.dma_start(fold_in[p][:], w_fold[bass.ds(n, 1)].rearrange("a p n -> (a p) n")).then_inc(loaded[p], 16)
                sp.dma_start(score_in[p][:], w_score[bass.ds(n, 1)].rearrange("a p n -> (a p) n")).then_inc(loaded[p], 16)

            pairs(sp, step)

        @block.tensor
        def _(pe):
            def step(i, p, n, first):
                pe.wait_ge(loaded[p], i * 32 + 32)
                if p == 0 and not first:
                    pe.wait_ge(copied_g, i * 2)
                    pe.wait_ge(copied_o, i * 2)
                for m in range(QT):
                    mm = nc.tensor.matmul(bank[2 * p][:, m * P:(m + 1) * P], score_in[p][:, m * P:(m + 1) * P],
                                          score_in[p][:, CQ:CQ + C], start=True, stop=True)
                mm.then_inc(made_g, 1)
                nc.tensor.matmul(bank[2 * p + 1][:], fold_in[p][:, 0:C], fold_in[p][:, C:C + D],
                                 start=True, stop=True).then_inc(made_o, 1)

            pairs(pe, step)

        @block.vector
        def _(dve):
            def step(i, p, n, first):
                dve.wait_ge(made_g, n + 1)
                if p == 0 and not first:
                    dve.wait_ge(folds_stored, i * 64)
                nc.vector.tensor_copy(fold_out[p][:, 0:CQ], bank[2 * p][:, 0:CQ]).then_inc(copied_g, 1)

            pairs(dve, step)

        @block.scalar
        def _(act):
            def step(i, p, n, first):
                act.wait_ge(made_o, n + 1)
                if p == 0 and not first:
                    act.wait_ge(folds_stored, i * 64)
                nc.scalar.activation(fold_out[p][:, CQ:CQ + D], bank[2 * p + 1][:], ACT.Copy).then_inc(copied_o, 1)
                act.wait_ge(copied_o, n + 1)
                act.wait_ge(copied_g, n + 1)
                act.dma_start(fold_g[bass.ds(n, 1)].rearrange("a p n -> (a p) n"), fold_out[p][:, 0:CQ]).then_inc(folds_stored, 16)
                act.dma_start(fold_o[bass.ds(n, 1)].rearrange("a p n -> (a p) n"), fold_out[p][:, CQ:CQ + D]).then_inc(folds_stored, 16)

            pairs(act, step)


def attention(nc, mem, sem, x, kv, w_first, fold_g, fold_o, rope_q, rope_k, folds_stored, x1_dram,
              x1_stored):
    sb = lambda name, shape, dt=F32: mem.enter_context(nc.sbuf_tensor(name, shape, dt))
    pair = lambda name, shape: (sb(name + "_hi", shape, F32R), sb(name + "_lo", shape, F32R))

    kvT = pair("kvT", [P, LT * P])
    kvl = pair("kvl", [P, LT, C])
    xnT = pair("xnT", [P, KD, S])
    wq = pair("wq", [P, WQ + CQ])
    wo = pair("wo", [P, D])
    qk = pair("qk", [P, S])
    qr = pair("qr", [P, QT, S])
    qc = [pair(f"qc{p}", [P, S]) for p in (0, 1)]
    ctxT = pair("ctxT", [P, S])
    e32 = [sb(f"e32_{p}", [P, L + 1]) for p in (0, 1)]
    x1 = sb("x1", [P, ST, D])
    xn = [sb(f"xn{p}", [P, D]) for p in (0, 1)]
    kv_in = sb("kv_in", [P, LT, C])
    wq_in = sb("wq_in", [P, WQ + CQ])
    wo_in = sb("wo_in", [P, D])
    cos_q = sb("cos_q", [P, QT, S])
    sin_q = sb("sin_q", [P, QT, S])
    straight = sb("straight", [P, QT, S])
    turned_q = sb("turned_q", [P, QT, S])
    ident = sb("ident", [P, P])
    mx = sb("mx", [P, 4])
    nmax = sb("nmax", [P, 2, ST])
    sums = sb("sums", [P, 2, ST, 4])
    rsum = sb("rsum", [P, 1])
    recip = sb("recip", [P, 2, ST])
    stats = sb("stats", [P, ST, 6])
    mv = sb("mv", [P, ST, 2])
    var = sb("var", [P, ST])
    std = sb("std", [P, ST])
    rstd = sb("rstd", [P, ST])
    with ExitStack() as shared:
        sh = lambda name, shape: shared.enter_context(nc.sbuf_tensor(name, shape, F32))
        cos_k, sin_k = sh("cos_k", [P, LT, C]), sh("sin_k", [P, LT, C])
        kv_r, kv_t = sh("kv_r", [P, LT, C]), sh("kv_t", [P, LT, C])
    eT = [pair(f"eT{f}", [P, LT, HW]) for f in (0, 1)]
    psum = lambda name, shape: mem.enter_context(nc.psum_tensor(name, shape, F32))
    score_bank = psum("score_bank", [P, 4, 512])
    turn_bank = [psum(f"turn_bank{i}", [P, 4, P]) for i in (0, 1)]
    ctx_bank = psum("ctx_bank", [P, S])
    item_bank = psum("item_bank", [P, 512])

    tables_in, kv_loaded, krope_in, x_in = sem("tables_in"), sem("kv_loaded"), sem("krope_in"), sem("x_in")
    wq_loaded, wo_loaded = sem("wq_loaded"), sem("wo_loaded")
    ident_zero, ident_ready, pad_ready = sem("ident_zero"), sem("ident_ready"), sem("pad_ready")
    stat_made, var_ready, eps_added, std_ready, rstd_ready, xn_ready = (sem("stat_made"), sem("var_ready"),
        sem("eps_added"), sem("std_ready"), sem("rstd_ready"), sem("xn_ready"))
    kv_mult, kv_roped, kv_hi, kv_lo = sem("kv_mult"), sem("kv_roped"), sem("kv_hi"), sem("kv_lo")
    pro_turned, pro_hi, pro_lo = sem("pro_turned"), sem("pro_hi"), sem("pro_lo")
    wq_hi, wq_lo, wo_hi, wo_lo = sem("wq_hi"), sem("wq_lo"), sem("wo_hi"), sem("wo_lo")
    scores_ready, max_part, nmax_ready = sem("scores_ready"), sem("max_part"), sem("nmax_ready")
    exp_done, sum_done, recip_done = sem("exp_done"), sem("sum_done"), sem("recip_done")
    e_turned, e_hi, e_lo = sem("e_turned"), sem("e_hi"), sem("e_lo")
    pv_done, ctx_hi, ctx_lo = sem("pv_done"), sem("ctx_hi"), sem("ctx_lo")
    qa_ready, qa_hi, qa_lo = sem("qa_ready"), sem("qa_hi"), sem("qa_lo")
    qb_ready, rope_mult, rope_sum = sem("qb_ready"), sem("rope_mult"), sem("rope_sum")
    rope_hi, rope_lo = sem("rope_hi"), sem("rope_lo")
    qc_ready, qc_hi, qc_lo = sem("qc_ready"), sem("qc_hi"), sem("qc_lo")
    op_ready, op_done = sem("op_ready"), sem("op_done")
    f32 = lambda ap: ap.bitcast(F32)

    with nc.Block() as block:

        @block.sync
        def _(sp):
            sp.dma_start(cos_q[:], rope_q[0]).then_inc(tables_in, 16)
            sp.dma_start(sin_q[:], rope_q[1]).then_inc(tables_in, 16)
            sp.wait_ge(pad_ready, 1)
            sp.wait_ge(folds_stored, 32 * H)
            one = lambda t, h: t[bass.ds(h, 1)].rearrange("a p n -> (a p) n")

            def load_batch(b, first):
                kv_b = kv[bass.ds(b, 1)]
                if not first:
                    sp.wait_ge(kv_mult, b * 3)
                sp.dma_start(kv_in[:, 0:LT - 1, :], kv_b[:, 0:(LT - 1) * P].rearrange("a (t p) c -> p (a t) c", p=P)).then_inc(kv_loaded, 16)
                sp.dma_start(kv_in[0:LR, LT - 1, :], kv_b[:, (LT - 1) * P:L].rearrange("a p c -> (a p) c")).then_inc(kv_loaded, 16)
                if not first:
                    sp.wait_ge(pv_done, b * 2 * H)
                sp.dma_start(cos_k[:], rope_k[0]).then_inc(krope_in, 16)
                sp.dma_start(sin_k[:], rope_k[1]).then_inc(krope_in, 16)
                if not first:
                    sp.wait_ge(x1_stored, b * 16)
                sp.dma_start(x1[:], x[bass.ds(b, 1)].rearrange("a (t p) d -> p (a t) d", p=P)).then_inc(x_in, 16)

                def load_first(h, free):
                    if free is not None:
                        sp.wait_ge(wq_lo, free)
                    sp.dma_start(wq_in[:, 0:WQ], one(w_first, h)).then_inc(wq_loaded, 16)
                    sp.dma_start(wq_in[:, WQ:WQ + CQ], one(fold_g, h)).then_inc(wq_loaded, 16)

                def load_out(h, free):
                    if free is not None:
                        sp.wait_ge(wo_lo, free)
                    sp.dma_start(wo_in[:], one(fold_o, h)).then_inc(wo_loaded, 16)

                load_first(0, None if first else b * H)
                load_first(1, b * H + 1)
                load_out(0, None if first else b * H)
                with sp.Fori(2, H) as h:
                    load_first(h, b * H + h)
                    load_out(h - 1, b * H + h - 1)
                load_out(H - 1, b * H + H - 1)

            load_batch(0, True)
            with sp.Fori(1, B) as b:
                load_batch(b, False)

        @block.gpsimd
        def _(pool):
            nc.gpsimd.memset(ident[:], 0.0).then_inc(ident_zero, 1)
            nc.gpsimd.memset(kv_in[:, LT - 1, :], 0.0).then_inc(pad_ready, 1)
            pool.wait_ge(ident_zero, 1)
            nc.gpsimd.affine_select(out=ident[:], in_=ident[:], compare_op=ALU.not_equal, fill=1.0, base=0,
                                    pattern=[[-1, P]], channel_multiplier=1).then_inc(ident_ready, 1)

            def low(out, full, high):
                return nc.gpsimd.tensor_tensor(out, full, f32(high), ALU.subtract)

            def first_low(n):
                pool.wait_ge(wq_hi, n + 1)
                low(wq[1][:], wq_in[:], wq[0][:]).then_inc(wq_lo, 1)

            def rope(n, m):
                pool.wait_ge(rope_mult, n * 3 + max(2, m + 1))
                nc.gpsimd.tensor_tensor(straight[:, m, :], straight[:, m, :], turned_q[:, m, :], ALU.add).then_inc(rope_sum, 1)

            def rope_low(n, m):
                pool.wait_ge(rope_hi, n * 3 + (m + 1))
                low(qr[1][:, m, :], straight[:, m, :], qr[0][:, m, :]).then_inc(rope_lo, 1)

            def head(at):
                n = at.n
                if at.has(1):
                    rope(n + 1, 0)
                    rope(n + 1, 1)
                    rope_low(n + 1, 0)
                    rope_low(n + 1, 1)
                    rope(n + 1, 2)
                    rope_low(n + 1, 2)
                if at.has(2):
                    first_low(n + 2)
                if at.has(0):
                    pool.wait_ge(wo_hi, n + 1)
                    low(wo[1][:], wo_in[:], wo[0][:]).then_inc(wo_lo, 1)

            with pool.Fori(0, B) as b:
                n0 = b * H
                first_low(n0)
                for m in range(QT):
                    rope(n0, m)
                    rope_low(n0, m)
                first_low(n0 + 1)
                heads_of(pool, b, head)

        @block.tensor
        def _(pe):
            def split_product(out, w, xx, first, last):
                nc.tensor.matmul(out, w[0], xx[0], start=first, stop=False)
                nc.tensor.matmul(out, w[0], xx[1], start=False, stop=False)
                return nc.tensor.matmul(out, w[1], xx[0], start=False, stop=last)

            def chain_a(n, part):
                if part[0] == 0:
                    pe.wait_ge(wq_lo, n + 1)
                for k in part:
                    w = [t[:, k * P:(k + 1) * P] for t in wq]
                    mm = split_product(item_bank[:], w, [t[:, k, :] for t in xnT], k == 0, k == KD - 1)
                if part[-1] == KD - 1:
                    mm.then_inc(qa_ready, 1)

            def chain_b(n, m):
                if m == 0:
                    pe.wait_ge(qa_lo, n + 1)
                else:
                    pe.wait_ge(rope_mult, n * 3 + m)
                w = [t[:, D + m * P:D + (m + 1) * P] for t in wq]
                split_product(item_bank[:], w, [t[:] for t in qk], True, True).then_inc(qb_ready, 1)

            def chain_c(n):
                pe.wait_ge(rope_mult, n * 3 + 3)
                for m in range(QT):
                    if m != 1:
                        pe.wait_ge(rope_lo, n * 3 + max(2, m + 1))
                    w = [t[:, WQ + m * P:WQ + (m + 1) * P] for t in wq]
                    mm = split_product(item_bank[:], w, [t[:, m, :] for t in qr], m == 0, m == QT - 1)
                mm.then_inc(qc_ready, 1)

            def scores(at, t, c):
                lo, width, _ = CHUNKS[c]
                if t == 0 and c == 0:
                    pe.wait_ge(qc_lo, at.n + 1)
                if t > 0 or at.h != 0:
                    pe.wait_ge(exp_done, at.n * 16 + (4 * t + c - 3))
                q = [w[:, t * P:(t + 1) * P] for w in qc[at.p]]
                split_product(score_bank[:, c, 0:width], q, [k[:, lo:lo + width] for k in kvT], True, True).then_inc(scores_ready, 1)

            def turn(n, h, t, g, added=None):
                if g < 3:
                    last_key = min((GROUPS[g][-1] + 1) * P, L)
                    pe.wait_ge(exp_done, n * 16 + (4 * t + -(-last_key // CH)))
                if not (h == 0 and t == 0 and g < 2):
                    pe.wait_ge(e_lo, n * 16 + (4 * t + g - 1))
                if added is not None:
                    pe.wait_ge(op_done, added)
                for i, lt in enumerate(GROUPS[g]):
                    rows = min(P, L - lt * P)
                    mm = nc.tensor.transpose(turn_bank[g % 2][0:rows, i, :], e32[t % 2][:, lt * P:lt * P + rows], ident[:])
                mm.then_inc(e_turned, 1)

            def context(n, half, part, first=False):
                out = ctx_bank[:, half * HW:(half + 1) * HW]
                if part == 0:
                    pe.wait_ge(e_lo, n * 16 + (8 * half + 8))
                    if not first:
                        pe.wait_ge(ctx_lo, n * 2 + half)
                kp, ep = ((0, 0), (0, 1), (1, 0))[part]
                for lt in range(LT):
                    rows = min(P, L - lt * P)
                    mm = nc.tensor.matmul(out, kvl[kp][0:rows, lt, :], eT[half][ep][0:rows, lt, :],
                                          start=(part == 0 and lt == 0), stop=(part == 2 and lt == LT - 1))
                if part == 2:
                    mm.then_inc(pv_done, 1)

            def project(at, j):
                n = at.n - 1
                if j == 0:
                    pe.wait_ge(wo_lo, n + 1)
                if j % 2 == 0:
                    pe.wait_ge(ctx_lo, n * 2 + (j // 2 + 1))
                if at.has(0):
                    pe.wait_ge(e_lo, at.n * 16 + ((j + 7) if j < 2 else (j + 9)))
                elif j >= 2:
                    pe.wait_ge(op_done, n * 4 + (j - 1))
                out = turn_bank[j % 2][:].rearrange("p k c -> p (k c)")
                split_product(out, [t[:, j * P:(j + 1) * P] for t in ctxT], [t[:] for t in wo], True, True).then_inc(op_ready, 1)

            def head(at):
                n = at.n
                for t in range(ST):
                    for c in range(4):
                        if at.has(0):
                            scores(at, t, c)
                        if t > 0 and at.has(0):
                            turn(n, at.h, t - 1, c, n * 4 + (c - 3) if t == 3 and c < 2 and at.has(-1) else None)
                        if t == 0 and at.has(-1):
                            turn(n - 1, None, ST - 1, c, n * 4 + (c - 5) if c < 2 and at.has(-2) else None)
                    if t == 0:
                        if at.has(-1):
                            context(n - 1, 0, 2)
                        if at.has(1):
                            chain_a(n + 1, range(0, KD))
                    if t == 1:
                        if at.has(1):
                            chain_b(n + 1, 0)
                        if at.has(-1):
                            context(n - 1, 1, 0)
                            context(n - 1, 1, 1)
                        if at.has(1):
                            chain_b(n + 1, 1)
                    if t == 2:
                        if at.has(-1):
                            context(n - 1, 1, 2)
                            project(at, 0)
                            project(at, 1)
                        if at.has(1):
                            chain_b(n + 1, 2)
                    if t == 3:
                        if at.has(1):
                            chain_c(n + 1)
                        if at.has(0):
                            context(n, 0, 0, at.h == 0)
                        if at.has(-1):
                            project(at, 2)
                            project(at, 3)
                        if at.has(0):
                            context(n, 0, 1)
            pe.wait_ge(ident_ready, 1)
            with pe.Fori(0, B) as b:
                for g in range(8):
                    if g >= 2:
                        pe.wait_ge(pro_lo, b * 8 + (g - 1))
                    if g < 4:
                        pe.wait_ge(xn_ready, b * 4 + (g + 1))
                        for k in range(KD):
                            mm = nc.tensor.transpose(turn_bank[g % 2][:, k, :], xn[g % 2][:, k * P:(k + 1) * P], ident[:])
                    else:
                        if g == 4:
                            pe.wait_ge(kv_roped, b + 1)
                        for i, lt in enumerate(GROUPS[g - 4]):
                            mm = nc.tensor.transpose(turn_bank[g % 2][:, i, :], kv_r[:, lt, :], ident[:])
                    mm.then_inc(pro_turned, 1)
                n0 = b * H
                pe.wait_ge(pro_lo, b * 8 + 8)
                chain_a(n0, range(KD))
                for m in range(QT):
                    chain_b(n0, m)
                chain_c(n0)
                pe.wait_ge(kv_lo, b + 1)
                heads_of(pe, b, head)

        @block.scalar
        def _(act):
            def hi(out, in_):
                return nc.scalar.activation(out, in_, ACT.Copy)

            def chain_hi(n, m):
                act.wait_ge(rope_sum, n * 3 + (m + 1))
                hi(qr[0][:, m, :], straight[:, m, :]).then_inc(rope_hi, 1)

            def turn_hi(n, h, t, g):
                act.wait_ge(e_turned, n * 16 + (4 * t + g + 1))
                half, k = t // 2, len(GROUPS[g])
                rows = P if g < 3 else LR
                if g == 0 and t % 2 == 0 and h != 0:
                    act.wait_ge(pv_done, n * 2 + (half - 1))
                hi(eT[half][0][0:rows, 4 * g:4 * g + k, (t % 2) * P:(t % 2 + 1) * P], turn_bank[g % 2][0:rows, 0:k, :]).then_inc(e_hi, 1)

            def context_hi(n, half):
                act.wait_ge(pv_done, n * 2 + (half + 1))
                cols = slice(half * HW, (half + 1) * HW)
                hi(ctxT[0][:, cols], ctx_bank[:, cols]).then_inc(ctx_hi, 1)

            def head(at):
                n = at.n
                for t in range(ST):
                    for g in range(4):
                        if t > 0 and at.has(0):
                            turn_hi(n, at.h, t - 1, g)
                        if t == 0 and at.has(-1):
                            turn_hi(n - 1, None, ST - 1, g)
                        if t == 3 and g == 1 and at.has(1):
                            chain_hi(n + 1, 2)
                    if t == 2 and at.has(1):
                        chain_hi(n + 1, 0)
                        chain_hi(n + 1, 1)
                    if t == 0 and at.has(-1):
                        context_hi(n - 1, 0)
                    if t == 3 and at.has(1):
                        act.wait_ge(qc_ready, n + 2)
                        hi(qc[1 - at.p][0][:], item_bank[:]).then_inc(qc_hi, 1)
                    if at.has(0):
                        act.wait_ge(nmax_ready, n * 4 + (t + 1))
                        for c, (lo, _, width) in enumerate(CHUNKS):
                            nc.scalar.activation(e32[t % 2][:, lo:lo + width], score_bank[:, c, 0:width], ACT.Exp,
                                                 bias=nmax[:, at.p, t:t + 1],
                                                 accum_out=sums[:, at.p, t, c:c + 1]).then_inc(exp_done, 1)
                    if t == 0 and at.has(1):
                        act.wait_ge(qa_ready, n + 2)
                        hi(qk[0][:], item_bank[:]).then_inc(qa_hi, 1)
                    if t == 2 and at.has(-1):
                        context_hi(n - 1, 1)
                    if t == 3 and at.has(2):
                        act.wait_ge(wq_loaded, n * 32 + 96)
                        hi(wq[0][:], wq_in[:]).then_inc(wq_hi, 1)
                    if t == 3 and at.has(0):
                        act.wait_ge(wo_loaded, n * 16 + 16)
                        if at.has(-1):
                            act.wait_ge(op_ready, n * 4)
                        hi(wo[0][:], wo_in[:]).then_inc(wo_hi, 1)

            with act.Fori(0, B) as b:
                n0 = b * H
                act.wait_ge(eps_added, b + 1)
                nc.scalar.activation(std[:], var[:], ACT.Sqrt).then_inc(std_ready, 1)
                act.wait_ge(wq_loaded, n0 * 32 + 32)
                hi(wq[0][:], wq_in[:]).then_inc(wq_hi, 1)
                for g in range(8):
                    act.wait_ge(pro_turned, b * 8 + (g + 1))
                    if g < 4:
                        hi(xnT[0][:, :, g * P:(g + 1) * P], turn_bank[g % 2][:]).then_inc(pro_hi, 1)
                    else:
                        k = len(GROUPS[g - 4])
                        lo = GROUPS[g - 4][0] * P
                        hi(kvT[0][:, lo:lo + k * P], turn_bank[g % 2][:, 0:k, :].rearrange("p k c -> p (k c)")).then_inc(pro_hi, 1)
                hi(kvl[0][:], kv_r[:]).then_inc(kv_hi, 1)
                act.wait_ge(qa_ready, n0 + 1)
                hi(qk[0][:], item_bank[:]).then_inc(qa_hi, 1)
                for m in range(QT):
                    chain_hi(n0, m)
                act.wait_ge(qc_ready, n0 + 1)
                hi(qc[0][0][:], item_bank[:]).then_inc(qc_hi, 1)
                act.wait_ge(wq_loaded, n0 * 32 + 64)
                hi(wq[0][:], wq_in[:]).then_inc(wq_hi, 1)
                heads_of(act, b, head)
                act.wait_ge(op_done, n0 * 4 + 4 * H)
                act.dma_start(x1_dram[:, bass.ds(b * ST, ST), :], x1[:]).then_inc(x1_stored, 16)

        @block.vector
        def _(dve):
            def low(out, full, high):
                return nc.vector.tensor_tensor(out, full, f32(high), ALU.subtract)

            def chain_rope(n, m, first=False):
                dve.wait_ge(qb_ready, n * 3 + (m + 1))
                if m == 0 and not first:
                    dve.wait_ge(rope_lo, n * 3)
                nc.vector.tensor_tensor(straight[:, m, :], item_bank[:], cos_q[:, m, :], ALU.mult)
                if m < 2:
                    nc.vector.tensor_tensor(turned_q[:, 1 - m, :], item_bank[:], sin_q[:, m, :], ALU.mult).then_inc(rope_mult, 1)
                else:
                    nc.vector.tensor_tensor(turned_q[64:P, m, :], item_bank[0:64, :], sin_q[0:64, m, :], ALU.mult)
                    nc.vector.tensor_tensor(turned_q[0:64, m, :], item_bank[64:P, :], sin_q[64:P, m, :], ALU.mult).then_inc(rope_mult, 1)

            def turn_lo(n, t, g):
                dve.wait_ge(e_hi, n * 16 + (4 * t + g + 1))
                half, k = t // 2, len(GROUPS[g])
                rows = P if g < 3 else LR
                cols = slice((t % 2) * P, (t % 2 + 1) * P)
                low(eT[half][1][0:rows, 4 * g:4 * g + k, cols], turn_bank[g % 2][0:rows, 0:k, :],
                    eT[half][0][0:rows, 4 * g:4 * g + k, cols]).then_inc(e_lo, 1)

            def reciprocal(n, p, t):
                dve.wait_ge(exp_done, n * 16 + (4 * t + 4))
                nc.vector.tensor_reduce(rsum[:], sums[:, p, t, :], AX.X, ALU.add).then_inc(sum_done, 1)
                dve.wait_ge(sum_done, n * 4 + (t + 1))
                nc.vector.reciprocal(recip[:, p, t:t + 1], rsum[:]).then_inc(recip_done, 1)

            def context_lo(n, half):
                dve.wait_ge(ctx_hi, n * 2 + (half + 1))
                cols = slice(half * HW, (half + 1) * HW)
                low(ctxT[1][:, cols], ctx_bank[:, cols], ctxT[0][:, cols]).then_inc(ctx_lo, 1)

            def add_output(n, p, j, first):
                dve.wait_ge(op_ready, n * 4 + (j + 1))
                if not first:
                    dve.wait_ge(op_done, n * 4 + (j - 3))
                out = turn_bank[j % 2][:].rearrange("p k c -> p (k c)")
                nc.vector.scalar_tensor_tensor(x1[:, j, :], out, recip[:, p, j:j + 1], x1[:, j, :],
                                               ALU.mult, ALU.add).then_inc(op_done, 1)

            def head(at):
                n = at.n
                for t in range(ST):
                    for c, (_, _, width) in enumerate(CHUNKS):
                        if at.has(0):
                            dve.wait_ge(scores_ready, n * 16 + (4 * t + c + 1))
                            nc.vector.tensor_reduce(mx[:, c:c + 1], score_bank[:, c, 0:width], AX.X, ALU.max).then_inc(max_part, 1)
                        if t > 0 and at.has(0):
                            turn_lo(n, t - 1, c)
                        if t == 0 and at.has(-1):
                            turn_lo(n - 1, ST - 1, c)
                    if at.has(0):
                        dve.wait_ge(max_part, n * 16 + (4 * t + 4))
                        nc.vector.tensor_reduce(nmax[:, at.p, t:t + 1], mx[:], AX.X, ALU.max, negate=True).then_inc(nmax_ready, 1)
                    if t > 0 and at.has(0):
                        reciprocal(n, at.p, t - 1)
                    if t == 0 and at.has(-1):
                        reciprocal(n - 1, 1 - at.p, ST - 1)
                    if t == 0 and at.has(-1):
                        context_lo(n - 1, 0)
                    if t == 0 and at.has(1):
                        dve.wait_ge(qa_hi, n + 2)
                        low(qk[1][:], item_bank[:], qk[0][:]).then_inc(qa_lo, 1)
                    if t == 1 and at.has(1):
                        chain_rope(n + 1, 0)
                        chain_rope(n + 1, 1)
                    if t == 2 and at.has(-1):
                        add_output(n - 1, 1 - at.p, 0, at.h == 1)
                        add_output(n - 1, 1 - at.p, 1, at.h == 1)
                    if t == 2:
                        if at.has(1):
                            chain_rope(n + 1, 2)
                        if at.has(-1):
                            context_lo(n - 1, 1)
                    if t == 3:
                        if at.has(1):
                            dve.wait_ge(qc_hi, n + 2)
                            low(qc[1 - at.p][1][:], item_bank[:], qc[1 - at.p][0][:]).then_inc(qc_lo, 1)
                        if at.has(-1):
                            add_output(n - 1, 1 - at.p, 2, at.h == 1)
                            add_output(n - 1, 1 - at.p, 3, at.h == 1)

            dve.wait_ge(tables_in, 32)
            with dve.Fori(0, B) as b:
                n0 = b * H
                dve.wait_ge(x_in, b * 16 + 16)
                for t in range(ST):
                    nc.vector.bn_stats(stats[:, t, :], x1[:, t, :]).then_inc(stat_made, 1)
                dve.wait_ge(stat_made, b * 4 + 4)
                nc.vector.memset(rsum[:], 0.0)
                for t in range(ST):
                    nc.vector.bn_aggr(mv[:, t, :], stats[:, t, :]).then_inc(var_ready, 1)
                dve.wait_ge(var_ready, b * 4 + 4)
                nc.vector.tensor_scalar(var[:], mv[:, :, 1], LN_EPS, None, ALU.add).then_inc(eps_added, 1)
                dve.wait_ge(std_ready, b + 1)
                nc.vector.reciprocal(rstd[:], std[:]).then_inc(rstd_ready, 1)
                dve.wait_ge(rstd_ready, b + 1)

                def norm(t):
                    if t >= 2:
                        dve.wait_ge(pro_turned, b * 8 + (t - 1))
                    nc.vector.tensor_scalar(xn[t % 2][:], x1[:, t, :], mv[:, t, 0:1], rstd[:, t:t + 1],
                                            ALU.subtract, ALU.mult).then_inc(xn_ready, 1)

                norm(0)
                norm(1)
                dve.wait_ge(kv_loaded, b * 32 + 32)
                dve.wait_ge(krope_in, b * 32 + 32)
                hc = C // 2
                nc.vector.tensor_tensor(kv_t[:, :, 0:hc], kv_in[:, :, hc:C], sin_k[:, :, 0:hc], ALU.mult).then_inc(kv_mult, 1)
                nc.vector.tensor_tensor(kv_t[:, :, hc:C], kv_in[:, :, 0:hc], sin_k[:, :, hc:C], ALU.mult).then_inc(kv_mult, 1)
                nc.vector.tensor_tensor(kv_r[:], kv_in[:], cos_k[:], ALU.mult).then_inc(kv_mult, 1)
                dve.wait_ge(kv_mult, b * 3 + 3)
                nc.vector.tensor_tensor(kv_r[:], kv_r[:], kv_t[:], ALU.add).then_inc(kv_roped, 1)
                for g in range(8):
                    dve.wait_ge(pro_hi, b * 8 + (g + 1))
                    if g < 4:
                        low(xnT[1][:, :, g * P:(g + 1) * P], turn_bank[g % 2][:], xnT[0][:, :, g * P:(g + 1) * P]).then_inc(pro_lo, 1)
                        if g < 2:
                            norm(g + 2)
                    else:
                        k = len(GROUPS[g - 4])
                        lo = GROUPS[g - 4][0] * P
                        low(kvT[1][:, lo:lo + k * P], turn_bank[g % 2][:, 0:k, :].rearrange("p k c -> p (k c)"),
                            kvT[0][:, lo:lo + k * P]).then_inc(pro_lo, 1)
                dve.wait_ge(kv_hi, b + 1)
                low(kvl[1][:], kv_r[:], kvl[0][:]).then_inc(kv_lo, 1)
                dve.wait_ge(qa_hi, n0 + 1)
                low(qk[1][:], item_bank[:], qk[0][:]).then_inc(qa_lo, 1)
                for m in range(QT):
                    chain_rope(n0, m, True)
                dve.wait_ge(qc_hi, n0 + 1)
                low(qc[0][1][:], item_bank[:], qc[0][0][:]).then_inc(qc_lo, 1)
                heads_of(dve, b, head)

def experts(nc, mem, sem, x1_dram, x1_stored, router_w, router_b, expert_w, expert_b, proj_w, proj_b,
            norm_w, iota, out):
    sb = lambda name, shape, dt=F32: mem.enter_context(nc.sbuf_tensor(name, shape, dt))
    pair = lambda name, shape: (sb(name + "_hi", shape, F32R), sb(name + "_lo", shape, F32R))
    ew = pair("ew", [P, E * KD, D])
    pw = pair("pw", [P, KD, D])
    rw = pair("rw", [P, KD, E])
    zT = [pair(f"zT{p}", [P, KD, P]) for p in (0, 1)]
    combT = pair("combT", [P, KD, P])
    stage = [sb(f"stage{i}", [P, 2, D]) for i in (0, 1)]
    eb, pb, nw, rb = sb("eb", [P, E, D]), sb("pb", [P, D]), sb("nw", [P, D]), sb("rb", [P, E])
    rw_in, lane, ident = sb("rw_in", [P, KD, E]), sb("lane", [P, E]), sb("ident2", [P, P])
    x_norm, x_res, z, y = sb("x_norm", [P, D]), sb("x_res", [P, D]), sb("z", [P, D]), sb("y", [P, D])
    hid = [sb(f"hid{i}", [P, D]) for i in (0, 1)]
    z_res = [sb(f"z_res{p}", [P, D]) for p in (0, 1)]
    comb = [sb(f"comb{p}", [P, D]) for p in (0, 1)]
    small = sb("small", [P, 64])
    col = lambda i, n=1: small[:, i:i + n]
    stats, mv, var, std, rstd = col(0, 6), col(6, 2), col(8), col(9), col(10)
    ss, ms, rms, rrms = col(11), col(12), col(13), col(14)
    diff, ratio, den, w1, w2, idxf = col(15), col(16), col(17), col(18), col(19), col(20, 2)
    logits, top, hot1, hot2 = col(24, 8), col(32, 8), col(40, 8), col(48, 8)
    idx = sb("idx", [P, 8], U32)
    full_w = [sb(f"full_w{p}", [P, E]) for p in (0, 1)]
    psum = lambda name, shape: mem.enter_context(nc.psum_tensor(name, shape, F32))
    hid_bank = [psum(f"hid_bank{i}", [P, D]) for i in range(4)]
    comb_bank, z_bank = psum("comb_bank", [P, KD, P]), psum("z_bank", [P, KD, P])
    proj_bank, router_bank = psum("proj_bank", [P, D]), psum("router_bank", [P, D])

    names = """small_in stage_in0 stage_in1 w_hi w_lo rw_hi rw_lo xn_in res_in res_ready id_zero id_ready
        z_stat z_mv z_var z_std z_rstd z_ready z_turned z_hi z_lo routed route_step diff_ready ratio_ready
        weights_ready hid_ready hid_added act_done comb_step comb_turned comb_hi comb_lo projected
        y_ready squared ms_ready rms_ready rrms_ready fin_ready out_ready out_stored""".split()
    s = {name: sem("x_" + name) for name in names}
    PIECES = E * KD // 2 + KD // 2
    piece = lambda t: (ew, t) if t < E * KD // 2 else (pw, t - E * KD // 2)
    tile_of = lambda n: (n // ST, n % ST)
    f32 = lambda ap: ap.bitcast(F32)

    with nc.Block() as block:

        @block.sync
        def _(sp):
            everyone = lambda v: v.rearrange("(a n) -> a n", a=1).broadcast_to([P, v.shape[0]])
            sp.dma_start(rw_in[:], router_w).then_inc(s["small_in"], 16)
            sp.dma_start(lane[:], iota).then_inc(s["small_in"], 16)
            sp.dma_start(rb[:], everyone(router_b)).then_inc(s["small_in"], 16)
            sp.dma_start(pb[:], everyone(proj_b)).then_inc(s["small_in"], 16)
            sp.dma_start(nw[:], everyone(norm_w)).then_inc(s["small_in"], 16)
            for e in range(E):
                sp.dma_start(eb[:, e, :], everyone(expert_b[e])).then_inc(s["small_in"], 16)
            x1_rows = x1_dram
            sp.wait_ge(x1_stored, 16 * B)
            sp.dma_start(x_norm[:], x1_rows[:, 0, :]).then_inc(s["xn_in"], 16)

            def load_norm(n):
                sp.wait_ge(s["z_ready"], n)
                sp.dma_start(x_norm[:], x1_rows[:, bass.ds(n, 1)].rearrange("p a d -> p (a d)")).then_inc(s["xn_in"], 16)

            for t in range(PIECES):
                if t == 2:
                    load_norm(1)
                if t >= 2:
                    sp.wait_ge(s["w_lo"], t - 1)
                src = expert_w[t // 2, :, (t % 2) * 2:(t % 2) * 2 + 2, :] if t < E * KD // 2 else \
                    proj_w[:, (t - E * KD // 2) * 2:(t - E * KD // 2) * 2 + 2, :]
                sp.dma_start(stage[t % 2][:], src).then_inc(s[f"stage_in{t % 2}"], 16)
            with sp.Fori(2, NT) as n:
                load_norm(n)

        @block.gpsimd
        def _(pool):
            nc.gpsimd.memset(ident[:], 0.0).then_inc(s["id_zero"], 1)
            pool.wait_ge(s["id_zero"], 1)
            nc.gpsimd.affine_select(out=ident[:], in_=ident[:], compare_op=ALU.not_equal, fill=1.0, base=0,
                                    pattern=[[-1, P]], channel_multiplier=1).then_inc(s["id_ready"], 1)
            pool.wait_ge(s["small_in"], 16 * (5 + E))
            x1_rows = x1_dram
            out_rows = out.rearrange("b s d -> (b s) d").rearrange("(n p) d -> p n d", p=P)
            one = lambda v, n: v[:, bass.ds(n, 1)].rearrange("p a d -> p (a d)")

            def store(n):
                pool.wait_ge(s["fin_ready"], n + 1)
                pool.wait_ge(s["res_in"], n * 16 + 16)
                nc.gpsimd.tensor_tensor(y[:], y[:], x_res[:], ALU.add).then_inc(s["out_ready"], 1)
                pool.wait_ge(s["out_ready"], n + 1)
                pool.dma_start(one(out_rows, n), y[:]).then_inc(s["out_stored"], 16)

            pool.wait_ge(s["z_ready"], 1)
            nc.gpsimd.tensor_tensor(z_res[0][:], z[:], pb[:], ALU.add).then_inc(s["res_ready"], 1)
            pool.dma_start(x_res[:], x1_rows[:, 0, :]).then_inc(s["res_in"], 16)
            pool.wait_ge(s["z_ready"], 2)
            nc.gpsimd.tensor_tensor(z_res[1][:], z[:], pb[:], ALU.add).then_inc(s["res_ready"], 1)
            with pool.Fori(0, NT // 2 - 1) as i:
                for p in (0, 1):
                    n = i * 2 + p
                    store(n)
                    pool.dma_start(x_res[:], one(x1_rows, n + 1)).then_inc(s["res_in"], 16)
                    pool.wait_ge(s["z_ready"], n + 3)
                    nc.gpsimd.tensor_tensor(z_res[p][:], z[:], pb[:], ALU.add).then_inc(s["res_ready"], 1)
            store(NT - 2)
            pool.dma_start(x_res[:], x1_rows[:, NT - 1, :]).then_inc(s["res_in"], 16)
            store(NT - 1)
            pool.wait_ge(s["out_stored"], 16 * NT)

        @block.tensor
        def _(pe):
            def split_product(out_ap, w, xx, first, last):
                nc.tensor.matmul(out_ap, w[0], xx[0], start=first, stop=False)
                nc.tensor.matmul(out_ap, w[0], xx[1], start=False, stop=False)
                return nc.tensor.matmul(out_ap, w[1], xx[0], start=False, stop=last)

            def turn(bank, src, done):
                for k in range(KD):
                    mm = nc.tensor.transpose(bank[:, k, :], src[:, k * P:(k + 1) * P], ident[:])
                mm.then_inc(done, 1)

            def over_width(bank, w, x_of, done):
                for k in range(KD):
                    mm = split_product(bank, [t[:, k, :] for t in w], x_of(k), k == 0, k == KD - 1)
                mm.then_inc(done, 1)

            def turn_z(n):
                pe.wait_ge(s["z_ready"], n + 1)
                turn(z_bank, z, s["z_turned"])

            def route(n, p):
                pe.wait_ge(s["z_lo"], n + 1)
                over_width(router_bank[:, 0:E], zT[p], lambda k: [t[:, k, :] for t in rw], s["routed"])

            def tile(at):
                n, p = at.n, at.p
                for e in range(E):
                    if at.has(0):
                        if at.h == 0:
                            pe.wait_ge(s["w_lo"], 2 * e + 2)
                        if at.h != 0 or e >= 4:
                            pe.wait_ge(s["hid_added"], n * E + (e - 3))
                        over_width(hid_bank[e % 4][:], zT[p], lambda k: [t[:, e * KD + k, :] for t in ew], s["hid_ready"])
                    if e == 2 and at.has(-1):
                        pe.wait_ge(s["comb_step"], n * E)
                        turn(comb_bank, comb[1 - p], s["comb_turned"])
                    if e == 3 and at.has(1):
                        turn_z(n + 1)
                    if e == 4 and at.has(-1):
                        if at.h == 1:
                            pe.wait_ge(s["w_lo"], PIECES)
                        pe.wait_ge(s["comb_lo"], n)
                        over_width(proj_bank[:], combT, lambda k: [t[:, k, :] for t in pw], s["projected"])
                    if e == 5 and at.has(1):
                        route(n + 1, 1 - p)

            pe.wait_ge(s["id_ready"], 1)
            turn_z(0)
            pe.wait_ge(s["rw_lo"], 1)
            route(0, 0)
            heads_of(pe, 0, tile)

        @block.scalar
        def _(act):
            def hi(out_ap, in_):
                return nc.scalar.activation(out_ap, in_, ACT.Copy)

            def z_root(n):
                act.wait_ge(s["z_var"], n + 1)
                nc.scalar.activation(std, var, ACT.Sqrt).then_inc(s["z_std"], 1)

            def z_high(n, p):
                act.wait_ge(s["z_turned"], n + 1)
                hi(zT[p][0][:], z_bank[:]).then_inc(s["z_hi"], 1)

            def ratio_of(n):
                act.wait_ge(s["diff_ready"], n + 1)
                nc.scalar.activation(ratio, diff, ACT.Exp).then_inc(s["ratio_ready"], 1)

            def tile(at):
                n, p = at.n, at.p
                for e in range(E):
                    if at.has(0):
                        act.wait_ge(s["hid_added"], n * E + (e + 1))
                        nc.scalar.activation(hid[e % 2][:], hid[e % 2][:], ACT.Silu).then_inc(s["act_done"], 1)
                    if e == 2 and at.has(-1):
                        act.wait_ge(s["comb_turned"], n)
                        hi(combT[0][:], comb_bank[:]).then_inc(s["comb_hi"], 1)
                    if e == 4 and at.has(1):
                        z_high(n + 1, 1 - p)
                    if e == 5 and at.has(-1):
                        act.wait_ge(s["y_ready"], n)
                        nc.scalar.activation(proj_bank[:], y[:], ACT.Square, accum_out=ss).then_inc(s["squared"], 1)
                    if e == 6 and at.has(1):
                        ratio_of(n + 1)
                    if e == 6 and at.has(-1):
                        act.wait_ge(s["ms_ready"], n)
                        nc.scalar.activation(rms, ms, ACT.Sqrt).then_inc(s["rms_ready"], 1)
                    if e == 6 and at.has(2):
                        z_root(n + 2)

            act.wait_ge(s["small_in"], 16 * (5 + E))
            hi(rw[0][:], rw_in[:]).then_inc(s["rw_hi"], 1)
            z_root(0)
            z_high(0, 0)
            z_root(1)
            ratio_of(0)
            for t in range(PIECES):
                w, r = piece(t)
                act.wait_ge(s[f"stage_in{t % 2}"], 16 * (t // 2 + 1))
                hi(w[0][:, 2 * r:2 * r + 2, :], stage[t % 2][:]).then_inc(s["w_hi"], 1)
            heads_of(act, 0, tile)

        @block.vector
        def _(dve):
            def low(out_ap, full, high):
                return nc.vector.tensor_tensor(out_ap, full, f32(high), ALU.subtract)

            def z_stats(n):
                dve.wait_ge(s["xn_in"], n * 16 + 16)
                nc.vector.bn_stats(stats, x_norm[:]).then_inc(s["z_stat"], 1)
                dve.wait_ge(s["z_stat"], n + 1)
                nc.vector.memset(col(56), 0.0)
                nc.vector.bn_aggr(mv, stats).then_inc(s["z_mv"], 1)
                dve.wait_ge(s["z_mv"], n + 1)
                nc.vector.tensor_scalar(var, small[:, 7:8], LN_EPS, None, ALU.add).then_inc(s["z_var"], 1)

            def z_norm(n):
                dve.wait_ge(s["z_std"], n + 1)
                nc.vector.reciprocal(rstd, std).then_inc(s["z_rstd"], 1)
                dve.wait_ge(s["z_rstd"], n + 1)
                dve.wait_ge(s["z_turned"], n)
                dve.wait_ge(s["res_ready"], n)
                nc.vector.tensor_scalar(z[:], x_norm[:], small[:, 6:7], rstd, ALU.subtract, ALU.mult).then_inc(s["z_ready"], 1)

            def z_low(n, p):
                dve.wait_ge(s["z_hi"], n + 1)
                low(zT[p][1][:], z_bank[:], zT[p][0][:]).then_inc(s["z_lo"], 1)

            def pick(n):
                def step(i, ins):
                    ins.then_inc(s["route_step"], 1)
                    dve.wait_ge(s["route_step"], n * 9 + (i + 1))
                dve.wait_ge(s["routed"], n + 1)
                step(0, nc.vector.tensor_tensor(logits, router_bank[:, 0:E], rb[:], ALU.add))
                nc.vector.memset(col(57), 0.0)
                step(1, nc.vector.max(top, logits))
                nc.vector.tensor_tensor(diff, small[:, 33:34], small[:, 32:33], ALU.subtract).then_inc(s["diff_ready"], 1)
                step(2, nc.vector.max_index(idx[:], top, logits))
                step(3, nc.vector.tensor_copy(idxf, idx[:, 0:2]))
                nc.vector.tensor_scalar(hot1, lane[:], small[:, 20:21], None, ALU.is_equal)
                step(4, nc.vector.tensor_scalar(hot2, lane[:], small[:, 21:22], None, ALU.is_equal))

            def weigh(n, p):
                def step(i, ins):
                    ins.then_inc(s["route_step"], 1)
                    dve.wait_ge(s["route_step"], n * 9 + (i + 1))
                dve.wait_ge(s["ratio_ready"], n + 1)
                step(5, nc.vector.tensor_scalar(den, ratio, 1.0, None, ALU.add))
                step(6, nc.vector.reciprocal(w1, den))
                step(7, nc.vector.tensor_tensor(w2, ratio, w1, ALU.mult))
                step(8, nc.vector.tensor_scalar(hot1, hot1, w1, None, ALU.mult))
                nc.vector.scalar_tensor_tensor(full_w[p][:], hot2, w2, hot1, ALU.mult, ALU.add).then_inc(s["weights_ready"], 1)

            def combine(at, e):
                n, p = at.n, at.p
                dve.wait_ge(s["act_done"], n * E + (e + 1))
                w = full_w[p][:, e:e + 1]
                if e == 0:
                    dve.wait_ge(s["weights_ready"], n + 1)
                    nc.vector.tensor_scalar(comb[p][:], hid[0][:], w, None, ALU.mult).then_inc(s["comb_step"], 1)
                else:
                    dve.wait_ge(s["comb_step"], n * E + e)
                    nc.vector.scalar_tensor_tensor(comb[p][:], hid[e % 2][:], w, comb[p][:], ALU.mult, ALU.add).then_inc(s["comb_step"], 1)

            def tile(at):
                n, p = at.n, at.p
                for e in range(E):
                    if at.has(0):
                        dve.wait_ge(s["hid_ready"], n * E + (e + 1))
                        if at.h != 0 or e >= 2:
                            dve.wait_ge(s["comb_step"], n * E + (e - 1))
                        nc.vector.tensor_tensor(hid[e % 2][:], hid_bank[e % 4][:], eb[:, e, :], ALU.add).then_inc(s["hid_added"], 1)
                        if e >= 1:
                            combine(at, e - 1)
                    if e == 2 and at.has(1):
                        z_norm(n + 1)
                    if e == 2 and at.has(-1):
                        dve.wait_ge(s["comb_hi"], n)
                        low(combT[1][:], comb_bank[:], combT[0][:]).then_inc(s["comb_lo"], 1)
                    if e == 4 and at.has(1):
                        z_low(n + 1, 1 - p)
                    if e == 5 and at.has(-1):
                        dve.wait_ge(s["projected"], n)
                        dve.wait_ge(s["res_ready"], n)
                        if at.has(-2):
                            dve.wait_ge(s["out_stored"], n * 16 - 16)
                        nc.vector.tensor_tensor(y[:], proj_bank[:], z_res[1 - p][:], ALU.add).then_inc(s["y_ready"], 1)
                    if e == 6 and at.has(-1):
                        dve.wait_ge(s["squared"], n)
                        nc.vector.tensor_scalar(ms, ss, 1.0 / D, RMS_EPS, ALU.mult, ALU.add).then_inc(s["ms_ready"], 1)
                    if e == 5 and at.has(2):
                        z_stats(n + 2)
                    if e == 6 and at.has(1):
                        pick(n + 1)
                    if e == 7 and at.has(1):
                        weigh(n + 1, 1 - p)
                    if e == 7 and at.has(-1):
                        dve.wait_ge(s["rms_ready"], n)
                        nc.vector.reciprocal(rrms, rms).then_inc(s["rrms_ready"], 1)
                        dve.wait_ge(s["rrms_ready"], n)
                        nc.vector.scalar_tensor_tensor(y[:], y[:], rrms, nw[:], ALU.mult, ALU.mult).then_inc(s["fin_ready"], 1)
                if at.has(0):
                    combine(at, E - 1)

            dve.wait_ge(s["rw_hi"], 1)
            low(rw[1][:], rw_in[:], rw[0][:]).then_inc(s["rw_lo"], 1)
            z_stats(0)
            z_norm(0)
            z_low(0, 0)
            z_stats(1)
            pick(0)
            weigh(0, 0)
            for t in range(PIECES):
                w, r = piece(t)
                dve.wait_ge(s["w_hi"], t + 1)
                low(w[1][:, 2 * r:2 * r + 2, :], stage[t % 2][:], w[0][:, 2 * r:2 * r + 2, :]).then_inc(s["w_lo"], 1)
            heads_of(dve, 0, tile)



def _rope(length, dim):
    inv = np.float32(1.0) / np.float32(10000.0) ** (np.arange(0, dim, 2, dtype=np.float32) / np.float32(dim))
    f = np.arange(length, dtype=np.float32)[:, None] * inv[None, :].astype(np.float32)
    return np.repeat(np.sin(f), 2, axis=-1), np.repeat(np.cos(f), 2, axis=-1)


def _layout(inputs):
    a = {k: np.asarray(v) for k, v in inputs.items()}
    order = np.r_[0:128, 192:320, 128:192, 320:384]
    wq = a["L0_xattn_Wq"].reshape(H, K, KD, P).transpose(0, 3, 2, 1).reshape(H, P, D)
    w_first = np.concatenate([wq, a["L0_xattn_w_kc_q"][:, :, order]], axis=2)
    wo = a["L0_xattn_Wo"].reshape(D, H, K).transpose(1, 2, 0)
    w_fold = np.concatenate([a["L0_xattn_w_kc_kv"], wo], axis=2)
    w_score = np.concatenate([a["L0_xattn_W_qr"][:, order, :].transpose(0, 2, 1),
                              a["L0_xattn_W_kr"].transpose(0, 2, 1)], axis=2)
    sin, cos = _rope(S, CQ)
    pack = lambda t: t.T.reshape(QT, P, S).transpose(1, 0, 2)
    partner = np.r_[192:320, 0:128, 320:384, 128:192]
    sign = np.r_[np.ones(128), -np.ones(128), np.ones(64), -np.ones(64)].astype(np.float32)
    rope_q = np.stack([pack(cos[:, order]), pack(sin[:, partner] * sign)])
    sin, cos = _rope(L, C)
    sin = sin * np.r_[-np.ones(C // 2), np.ones(C // 2)].astype(np.float32)
    pad = lambda t: np.concatenate([t, np.zeros((LT * P - L, C), np.float32)]).reshape(LT, P, C).transpose(1, 0, 2)
    rope_k = np.stack([pad(cos), pad(sin)])
    ew = a["L0_ffn_expert_w"].reshape(E, KD, P, D).transpose(0, 2, 1, 3)
    pw = a["L0_ffn_proj_w"].reshape(KD, P, D).transpose(1, 0, 2)
    rw = a["L0_ffn_router_w"].reshape(KD, P, E).transpose(1, 0, 2)
    iota = np.broadcast_to(np.arange(E, dtype=np.float32), (P, E))
    return {"x": a["x"], "kv": a["ctx_512"], "w_first": w_first, "w_fold": w_fold, "w_score": w_score,
            "router_w": rw, "router_b": a["L0_ffn_router_b"], "expert_w": ew, "expert_b": a["L0_ffn_expert_b"],
            "proj_w": pw, "proj_b": a["L0_ffn_proj_b"], "norm_w": a["L0_ffn_norm_w"],
            "rope_q": rope_q.astype(np.float32), "rope_k": rope_k.astype(np.float32), "iota": iota}


def kernel(**inputs):
    import concourse.bacc as _bacc
    from concourse.bass_utils import run_bass_kernel_spmd as _run

    nc = _bacc.Bacc("TRN2", target_bir_lowering=False, num_devices=1)
    arrays = {f"in_{k}": np.ascontiguousarray(v) for k, v in _layout(inputs).items()}
    args = [nc.dram_tensor(k, v.shape, mybir.dt.from_np(v.dtype), kind="ExternalInput").ap()
            for k, v in arrays.items()]
    args.append(nc.dram_tensor("out_dram", (B, S, D), F32, kind="ExternalOutput").ap())
    build(nc, *args)
    return _run(nc, [arrays], core_ids=[0]).results[0]["out_dram"]
```

```python
from contextlib import ExitStack

import numpy as np

import concourse.bass as bass
from concourse import mybir

F32 = mybir.dt.float32
F32R = mybir.dt.float32r
U32 = mybir.dt.uint32
ACT = mybir.ActivationFunctionType
ALU = mybir.AluOpType
AX = mybir.AxisListType

P = 128
B, S, D = 4, 512, 512
L, C = 1601, 128
H, K, CQ, R = 16, 128, 384, 64
E = 8
LT = (L + P - 1) // P
LR = L - (LT - 1) * P
ST = S // P
KD = D // P
QT = CQ // P
CH = 402
CHUNKS = [(c * CH, min(CH, L + 1 - c * CH), min(CH, L - c * CH)) for c in range(4)]
GROUPS = [range(4 * g, min(4 * g + 4, LT)) for g in range(4)]
HW = S // 2
NT = B * ST
LN_EPS, RMS_EPS = 1e-5, 1e-6
WQ = D + CQ
OUT_STAGE = (2, 2, 3, 3)

EARLY = {"ew": [P, E * KD, D], "eb": [P, E, D], "pb": [P, D], "nw": [P, D], "x_norm": [P, D],
         "rw_in": [P, KD, E], "rb": [P, E], "lane": [P, E]}


class Place:

    def __init__(self, h, n, p, fold, stored=None, next_batch=None):
        self.h, self.n, self.p, self.fold, self.stored, self.next_batch = h, n, p, fold, stored, next_batch

    def has(self, d):
        return self.h is None or 0 <= self.h + d < H


def heads_of(eng, b, step, first=True, last=True):
    n0 = b * H
    for h in (0, 1):
        step(Place(h, n0 + h, h % 2, first, stored=None if first else b))
    with eng.Fori(1, H // 2 - 1) as i:
        for p in (0, 1):
            step(Place(None, n0 + i * 2 + p, p, first))
    for h in range(H - 2, H + 1):
        step(Place(h, n0 + h, h % 2, first, next_batch=None if last else b + 1))


def batches(eng, step):
    step(0, True, False)
    with eng.Fori(1, B - 1) as b:
        step(b, False, False)
    step(B - 1, False, True)


def build(nc, x, kv, w_first, w_fold, w_score, router_w, router_b, expert_w, expert_b, proj_w,
          proj_b, norm_w, rope_q, rope_k, iota, out):
    with ExitStack() as ctx:
        sem = lambda name: ctx.enter_context(nc.semaphore(name))
        x1_dram = nc.dram_tensor("x1_scratch", (P, NT, D), F32).ap()
        fold_g = nc.dram_tensor("g_scratch", (H, P, CQ), F32).ap()
        fold_o = nc.dram_tensor("wo_scratch", (H, P, D), F32).ap()
        x1_stored = sem("x1_stored")
        with ExitStack() as mem:
            early = {name: mem.enter_context(nc.sbuf_tensor("early_" + name, shape, F32))
                     for name, shape in EARLY.items()}
        everyone = lambda v: v.rearrange("(a n) -> a n", a=1).broadcast_to([P, v.shape[0]])
        expert_inputs = [(early["x_norm"][:], x1_dram[:, 0, :]), (early["rw_in"][:], router_w),
                         (early["lane"][:], iota), (early["rb"][:], everyone(router_b)),
                         (early["pb"][:], everyone(proj_b)), (early["nw"][:], everyone(norm_w))]
        experts_in = sem("experts_in")
        weights_in = [sem(f"expert_weights_in{e}") for e in range(E)]
        for e in range(E):
            expert_inputs.append((early["eb"][:, e, :], everyone(expert_b[e])))
        expert_inputs = [(place, src, experts_in) for place, src in expert_inputs]
        for e in range(E):
            expert_inputs.append((early["ew"][:, e * KD:(e + 1) * KD, :], expert_w[e], weights_in[e]))
        with ExitStack() as mem:
            attention(nc, mem, sem, x, kv, w_first, w_fold, w_score, fold_g, fold_o, rope_q, rope_k,
                      x1_dram, x1_stored, expert_inputs)
        with ExitStack() as mem:
            kept = [mem.enter_context(nc.sbuf_tensor("kept_" + name, shape, F32R if name == "ew" else F32))
                    for name, shape in EARLY.items()]
            experts(nc, mem, sem, x1_dram, x1_stored, early, kept[0], experts_in, weights_in, proj_w, out)


def attention(nc, mem, sem, x, kv, w_first, w_fold, w_score, fold_g, fold_o, rope_q, rope_k, x1_dram,
              x1_stored, expert_inputs):
    sb = lambda name, shape, dt=F32: mem.enter_context(nc.sbuf_tensor(name, shape, dt))
    pair = lambda name, shape: (sb(name + "_hi", shape, F32R), sb(name + "_lo", shape, F32R))

    with ExitStack() as shared:
        kv_in = shared.enter_context(nc.sbuf_tensor("kv_in", [P, LT, C], F32))
    xnT = pair("xnT", [P, KD, S])
    wq = pair("wq", [P, D])
    wr = pair("wr", [P, 2 * CQ])
    qk = pair("qk", [P, S])
    qr = pair("qr", [P, QT, S])
    x_next = sb("x_next", [P, ST, D])
    trig_k = sb("trig_k", [P, 2, LT, C // 2])
    cos_q = sb("cos_q", [P, QT, S])
    sin_q = sb("sin_q", [P, QT, S])
    straight = sb("straight", [P, QT, S])
    turned_q = sb("turned_q", [P, QT, S])
    with ExitStack() as shared:
        fold_in = shared.enter_context(nc.sbuf_tensor("fold_in", [P, C + D], F32))
        score_in = shared.enter_context(nc.sbuf_tensor("score_in", [R, CQ + C], F32))
    xn = [sb(f"xn{p}", [P, D]) for p in (0, 1)]
    sb("fold_rest", [P, C + D + CQ + C - 2 * D])
    wq_in = sb("wq_in", [P, D])
    wr_in = sb("wr_in", [P, 2 * CQ])

    kvT = pair("kvT", [P, LT * P])
    kvl = pair("kvl", [P, LT, C])
    wo = pair("wo", [P, D])
    qc = [pair(f"qc{p}", [P, S]) for p in (0, 1)]
    ctxT = pair("ctxT", [P, S])
    e32 = [sb(f"e32_{p}", [P, L + 1]) for p in (0, 1)]
    x1 = sb("x1", [P, ST, D])
    wo_in = sb("wo_in", [P, D])
    ident = sb("ident", [P, P])
    mx = sb("mx", [P, 4])
    nmax = sb("nmax", [P, 2, ST])
    sums = sb("sums", [P, 2, ST, 4])
    rsum = sb("rsum", [P, ST])
    recip = sb("recip", [P, 2, ST])
    stats = sb("stats", [P, ST, 6])
    mv = sb("mv", [P, ST, 2])
    var = sb("var", [P, ST])
    std = sb("std", [P, ST])
    rstd = sb("rstd", [P, ST])
    with ExitStack() as shared:
        sh = lambda name, shape: shared.enter_context(nc.sbuf_tensor(name, shape, F32))
        kv_r, kv_t = sh("kv_r", [P, LT, C]), sh("kv_t", [P, LT, C])
    eT = [pair(f"eT{f}", [P, LT, HW]) for f in (0, 1)]
    psum = lambda name, shape: mem.enter_context(nc.psum_tensor(name, shape, F32))
    score_bank = psum("score_bank", [P, 4, 512])
    turn_bank = [psum(f"turn_bank{i}", [P, 4, P]) for i in (0, 1)]
    ctx_bank = psum("ctx_bank", [P, S])
    item_bank = psum("item_bank", [P, 512])

    tables_in, kv_loaded, x_in = sem("tables_in"), sem("kv_loaded"), sem("x_in")
    rotary_in = sem("rotary_in")
    score_loaded, fold_loaded = sem("score_loaded"), sem("fold_loaded")
    made_g, made_o, copied_g, copied_o = sem("made_g"), sem("made_o"), sem("copied_g"), sem("copied_o")
    g_stored, o_stored = sem("g_stored"), sem("o_stored")
    wq_loaded, wr_loaded, wo_loaded = sem("wq_loaded"), sem("wr_loaded"), sem("wo_loaded")
    ident_zero, ident_ready, pad_ready = sem("ident_zero"), sem("ident_ready"), sem("pad_ready")
    stat_made, var_ready, eps_added, std_ready, rstd_ready, xn_ready = (sem("stat_made"), sem("var_ready"),
        sem("eps_added"), sem("std_ready"), sem("rstd_ready"), sem("xn_ready"))
    kv_mult, kv_roped, kv_hi, kv_lo = sem("kv_mult"), sem("kv_roped"), sem("kv_hi"), sem("kv_lo")
    pro_turned, pro_hi, pro_lo = sem("pro_turned"), sem("pro_hi"), sem("pro_lo")
    wq_hi, wq_lo, wo_hi, wo_lo = sem("wq_hi"), sem("wq_lo"), sem("wo_hi"), sem("wo_lo")
    wr_hi, wr_lo = sem("wr_hi"), sem("wr_lo")
    scores_ready, max_part, nmax_ready = sem("scores_ready"), sem("max_part"), sem("nmax_ready")
    exp_done, sum_done, recip_done = sem("exp_done"), sem("sum_done"), sem("recip_done")
    e_turned, e_hi, e_lo = sem("e_turned"), sem("e_hi"), sem("e_lo")
    pv_done, ctx_hi, ctx_lo = sem("pv_done"), sem("ctx_hi"), sem("ctx_lo")
    qa_ready, qa_hi, qa_lo = sem("qa_ready"), sem("qa_hi"), sem("qa_lo")
    qb_ready, rope_mult, rope_sum = sem("qb_ready"), sem("rope_mult"), sem("rope_sum")
    rope_hi, rope_lo = sem("rope_hi"), sem("rope_lo")
    qc_ready, qc_hi, qc_lo = sem("qc_ready"), sem("qc_hi"), sem("qc_lo")
    op_ready, op_done = sem("op_ready"), sem("op_done")
    f32 = lambda ap: ap.bitcast(F32)

    with nc.Block() as block:

        @block.sync
        def _(sp):
            one = lambda t, h: t[bass.ds(h, 1)].rearrange("a p n -> (a p) n")

            def load_inputs(b, first):
                if not first:
                    sp.wait_ge(op_done, b * 64 - 60)
                sp.dma_start(x_next[:], x[bass.ds(b, 1)].rearrange("a (t p) d -> p (a t) d", p=P)).then_inc(x_in, 16)
                if first:
                    sp.dma_start(trig_k[:], rope_k).then_inc(rotary_in, 16)
                sp.wait_ge(pad_ready, b + 1)
                kv_b = kv[bass.ds(b, 1)]
                sp.dma_start(kv_in[:, 0:LT - 1, :], kv_b[:, 0:(LT - 1) * P].rearrange("a (t p) c -> p (a t) c", p=P)).then_inc(kv_loaded, 16)
                sp.dma_start(kv_in[0:LR, LT - 1, :], kv_b[:, (LT - 1) * P:L].rearrange("a p c -> (a p) c")).then_inc(kv_loaded, 16)

            def load_weights(b, first, last):
                if first:
                    return load_and_fold()
                def load_query(h, free):
                    sp.wait_ge(wq_lo, free)
                    sp.dma_start(wq_in[:], one(w_first, h)[:, 0:D]).then_inc(wq_loaded, 16)

                def load_rotary(h, free):
                    sp.wait_ge(wr_lo, free)
                    sp.dma_start(wr_in[:, 0:CQ], one(w_first, h)[:, D:WQ]).then_inc(wr_loaded, 16)
                    sp.dma_start(wr_in[:, CQ:2 * CQ], one(fold_g, h)).then_inc(wr_loaded, 16)

                def load_out(h, free):
                    sp.wait_ge(wo_lo, free)
                    sp.dma_start(wo_in[:], one(fold_o, h)).then_inc(wo_loaded, 16)

                n0 = b * H
                sp.wait_ge(g_stored, H * 16)
                sp.wait_ge(o_stored, H * 16)
                load_query(0, n0)
                load_rotary(0, n0)
                load_query(1, n0 + 1)
                load_rotary(1, n0 + 1)
                load_query(2, n0 + 2)
                load_rotary(2, n0 + 2)
                load_query(3, n0 + 3)
                load_out(0, n0)
                with sp.Fori(2, H - 2) as h:
                    load_rotary(h + 1, n0 + h + 1)
                    load_query(h + 2, n0 + h + 2)
                    load_out(h - 1, n0 + h - 1)
                load_rotary(H - 1, n0 + H - 1)
                load_out(H - 3, n0 + H - 3)
                load_out(H - 2, n0 + H - 2)
                if not last:
                    load_inputs(b + 1, False)
                load_out(H - 1, n0 + H - 1)

            def load_and_fold():
                def load_query(h):
                    sp.wait_ge(wq_lo, h)
                    sp.dma_start(wq_in[:], one(w_first, h)[:, 0:D]).then_inc(wq_loaded, 16)

                def load_rotary(h):
                    sp.wait_ge(wr_lo, h)
                    sp.dma_start(wr_in[:, 0:CQ], one(w_first, h)[:, D:WQ]).then_inc(wr_loaded, 16)

                def load_score(h):
                    sp.wait_ge(made_g, h)
                    sp.dma_start(score_in[:], one(w_score, h)).then_inc(score_loaded, 16)

                def load_fold(h):
                    sp.wait_ge(made_o, h)
                    sp.dma_start(fold_in[:], one(w_fold, h)).then_inc(fold_loaded, 16)

                def store_g(h):
                    sp.wait_ge(copied_g, h + 1)
                    sp.dma_start(one(fold_g, h), wr_in[:, CQ:2 * CQ]).then_inc(g_stored, 16)

                def store_o(h):
                    sp.wait_ge(copied_o, h + 1)
                    sp.dma_start(one(fold_o, h), wo_in[:]).then_inc(o_stored, 16)

                def place(n, has):
                    if has(-1):
                        store_o(n - 1)
                        load_fold(n)
                    if has(2):
                        load_rotary(n + 2)
                        store_g(n + 2)
                    if has(3):
                        load_score(n + 3)
                        load_query(n + 3)

                sp.dma_start(wq_in[:], one(w_first, 0)[:, 0:D]).then_inc(wq_loaded, 16)
                sp.dma_start(wr_in[:, 0:CQ], one(w_first, 0)[:, D:WQ]).then_inc(wr_loaded, 16)
                sp.wait_ge(pro_turned, 4)
                sp.dma_start(score_in[:], one(w_score, 0)).then_inc(score_loaded, 16)
                sp.dma_start(fold_in[:], one(w_fold, 0)).then_inc(fold_loaded, 16)
                store_g(0)
                load_score(1)
                load_query(1)
                load_rotary(1)
                store_g(1)
                load_score(2)
                load_query(2)
                at = lambda h: lambda d: 0 <= h + d < H
                place(0, at(0))
                with sp.Fori(1, H - 3) as n:
                    place(n, lambda d: True)
                for h in range(H - 3, H):
                    place(h, at(h))
                load_inputs(1, False)
                store_o(H - 1)

            load_inputs(0, True)
            sp.dma_start(cos_q[:], rope_q[0]).then_inc(tables_in, 16)
            sp.dma_start(sin_q[:], rope_q[1]).then_inc(tables_in, 16)
            batches(sp, load_weights)
            sp.wait_ge(qc_lo, B * H)
            for place, src, arrived in expert_inputs:
                sp.dma_start(place, src).then_inc(arrived, 16)

        @block.gpsimd
        def _(pool):
            nc.gpsimd.memset(ident[:], 0.0).then_inc(ident_zero, 1)
            pool.wait_ge(ident_zero, 1)
            nc.gpsimd.affine_select(out=ident[:], in_=ident[:], compare_op=ALU.not_equal, fill=1.0, base=0,
                                    pattern=[[-1, P]], channel_multiplier=1).then_inc(ident_ready, 1)

            def low(out, full, high):
                return nc.gpsimd.tensor_tensor(out, full, f32(high), ALU.subtract)

            def first_low(n):
                pool.wait_ge(wq_hi, n + 1)
                low(wq[1][:], wq_in[:], wq[0][:]).then_inc(wq_lo, 1)

            def rotary_low(n):
                pool.wait_ge(wr_hi, n + 1)
                low(wr[1][:], wr_in[:], wr[0][:]).then_inc(wr_lo, 1)

            def rope(n, m):
                pool.wait_ge(rope_mult, n * 3 + max(2, m + 1))
                nc.gpsimd.tensor_tensor(straight[:, m, :], straight[:, m, :], turned_q[:, m, :], ALU.add).then_inc(rope_sum, 1)

            def rope_low(n, m):
                pool.wait_ge(rope_hi, n * 3 + (m + 1))
                low(qr[1][:, m, :], straight[:, m, :], qr[0][:, m, :]).then_inc(rope_lo, 1)

            def head(at):
                n = at.n
                if at.has(1):
                    rotary_low(n + 1)
                if at.has(-1):
                    pool.wait_ge(wo_hi, n)
                    low(wo[1][:], wo_in[:], wo[0][:]).then_inc(wo_lo, 1)
                if at.has(2):
                    first_low(n + 2)
                if at.has(1):
                    rope(n + 1, 0)
                    rope(n + 1, 1)
                    rope_low(n + 1, 0)
                    rope_low(n + 1, 1)
                    rope(n + 1, 2)
                    rope_low(n + 1, 2)

            def batch(b, first, last):
                n0 = b * H
                first_low(n0)
                rotary_low(n0)
                first_low(n0 + 1)
                rope_low(n0, 0)
                rope_low(n0, 1)
                heads_of(pool, b, head, first, last)

            batches(pool, batch)

        @block.tensor
        def _(pe):
            def split_product(out, w, xx, first, last):
                nc.tensor.matmul(out, w[0], xx[0], start=first, stop=False)
                nc.tensor.matmul(out, w[0], xx[1], start=False, stop=False)
                return nc.tensor.matmul(out, w[1], xx[0], start=False, stop=last)

            def chain_a(n):
                pe.wait_ge(wq_lo, n + 1)
                for k in range(KD):
                    w = [t[:, k * P:(k + 1) * P] for t in wq]
                    mm = split_product(item_bank[:], w, [t[:, k, :] for t in xnT], k == 0, k == KD - 1)
                mm.then_inc(qa_ready, 1)

            def chain_b(n, m):
                if m == 0:
                    pe.wait_ge(wr_lo, n + 1)
                    pe.wait_ge(qa_lo, n + 1)
                else:
                    pe.wait_ge(rope_mult, n * 3 + m)
                w = [t[:, m * P:(m + 1) * P] for t in wr]
                split_product(item_bank[:], w, [t[:] for t in qk], True, True).then_inc(qb_ready, 1)

            def chain_c(n):
                pe.wait_ge(rope_mult, n * 3 + 3)
                for m in range(QT):
                    if m != 1:
                        pe.wait_ge(rope_lo, n * 3 + max(2, m + 1))
                    w = [t[:, CQ + m * P:CQ + (m + 1) * P] for t in wr]
                    mm = split_product(item_bank[:], w, [t[:, m, :] for t in qr], m == 0, m == QT - 1)
                mm.then_inc(qc_ready, 1)

            def scores(at, t, c):
                lo, width, _ = CHUNKS[c]
                if t == 0 and c == 0:
                    pe.wait_ge(qc_lo, at.n + 1)
                if t > 0 or at.h != 0:
                    pe.wait_ge(exp_done, at.n * 16 + (4 * t + c - 3))
                q = [w[:, t * P:(t + 1) * P] for w in qc[at.p]]
                split_product(score_bank[:, c, 0:width], q, [k[:, lo:lo + width] for k in kvT], True, True).then_inc(scores_ready, 1)

            def turn(n, h, t, g, added=None):
                if g < 3:
                    last_key = min((GROUPS[g][-1] + 1) * P, L)
                    pe.wait_ge(exp_done, n * 16 + (4 * t + -(-last_key // CH)))
                if not (h == 0 and t == 0 and g < 2):
                    pe.wait_ge(e_lo, n * 16 + (4 * t + g - 1))
                if added is not None:
                    pe.wait_ge(op_done, added)
                for i, lt in enumerate(GROUPS[g]):
                    rows = min(P, L - lt * P)
                    mm = nc.tensor.transpose(turn_bank[g % 2][0:rows, i, :], e32[t % 2][:, lt * P:lt * P + rows], ident[:])
                mm.then_inc(e_turned, 1)

            def fold_score(n, bank):
                pe.wait_ge(score_loaded, n * 16 + 16)
                for m in range(QT):
                    mm = nc.tensor.matmul(bank[:, m * P:(m + 1) * P], score_in[:, m * P:(m + 1) * P],
                                          score_in[:, CQ:CQ + C], start=True, stop=True)
                mm.then_inc(made_g, 1)

            def fold_output(n):
                pe.wait_ge(fold_loaded, n * 16 + 16)
                pe.wait_ge(e_lo, n * 16 + 16)
                nc.tensor.matmul(turn_bank[1][:].rearrange("p k c -> p (k c)"), fold_in[:, 0:C], fold_in[:, C:C + D],
                                 start=True, stop=True).then_inc(made_o, 1)

            def context(n, half, part, first=False):
                out = ctx_bank[:, half * HW:(half + 1) * HW]
                if part == 0:
                    pe.wait_ge(e_lo, n * 16 + (8 * half + 8))
                    if not first:
                        pe.wait_ge(ctx_lo, n * 2 + half)
                kp, ep = ((0, 0), (0, 1), (1, 0))[part]
                for lt in range(LT):
                    rows = min(P, L - lt * P)
                    mm = nc.tensor.matmul(out, kvl[kp][0:rows, lt, :], eT[half][ep][0:rows, lt, :],
                                          start=(part == 0 and lt == 0), stop=(part == 2 and lt == LT - 1))
                if part == 2:
                    mm.then_inc(pv_done, 1)

            def project(at, j):
                n = at.n - 1
                if j == 0:
                    pe.wait_ge(wo_lo, n + 1)
                if j % 2 == 0:
                    pe.wait_ge(ctx_lo, n * 2 + (j // 2 + 1))
                if j == 1 and at.fold and not at.has(0):
                    pe.wait_ge(copied_o, n + 1)
                if at.has(0) or OUT_STAGE[j] == 0:
                    pe.wait_ge(e_lo, at.n * 16 + (4 * OUT_STAGE[j] - 1 + j % 2))
                elif j >= 2:
                    pe.wait_ge(op_done, n * 4 + (j - 1))
                out = turn_bank[j % 2][:].rearrange("p k c -> p (k c)")
                split_product(out, [t[:, j * P:(j + 1) * P] for t in ctxT], [t[:] for t in wo], True, True).then_inc(op_ready, 1)

            def outputs_before(n, t, bank, any_before):
                before, heads = (t - 1, 1) if t > 0 else (ST - 1, 2)
                those = [j for j in range(ST) if OUT_STAGE[j] == before and j % 2 == bank]
                return n * 4 + (those[-1] + 1 - heads * 4) if those and any_before else None

            def head(at):
                n = at.n
                for t in range(ST):
                    for c in range(4):
                        if at.has(0):
                            scores(at, t, c)
                        if t == 1 and c == 1 and at.fold and at.has(0) and at.has(-1):
                            pe.wait_ge(copied_o, n)
                        if t == 2 and c == 0 and at.fold and at.has(2):
                            pe.wait_ge(copied_g, n + 3)
                        if t > 0 and at.has(0):
                            turn(n, at.h, t - 1, c, outputs_before(n, t, c, at.has(-1)))
                        if t == 0 and at.has(-1):
                            turn(n - 1, None, ST - 1, c, outputs_before(n, 0, c, at.has(-2)))
                    if t == 0:
                        if at.has(-1):
                            context(n - 1, 0, 2)
                            if at.fold:
                                fold_output(n - 1)
                        if at.has(1):
                            chain_a(n + 1)
                    if t == 1:
                        if at.has(1):
                            chain_b(n + 1, 0)
                        if at.has(2) and at.fold:
                            pe.wait_ge(e_lo, n * 16 + 3)
                            fold_score(n + 2, turn_bank[0][:].rearrange("p k c -> p (k c)"))
                        if at.has(-1):
                            context(n - 1, 1, 0)
                            context(n - 1, 1, 1)
                        if at.has(1):
                            chain_b(n + 1, 1)
                        if at.has(-1):
                            context(n - 1, 1, 2)
                    if t == 2:
                        if at.has(1):
                            chain_b(n + 1, 2)
                        if at.has(-1):
                            project(at, 0)
                            project(at, 1)
                        if at.has(0):
                            context(n, 0, 0, at.h == 0)
                    if t == 3:
                        if at.has(1):
                            chain_c(n + 1)
                        if at.has(-1):
                            project(at, 2)
                            project(at, 3)
                        if at.has(0):
                            context(n, 0, 1)
            def turn_inputs(b, first, g):
                if g >= 2:
                    pe.wait_ge(pro_lo, b * 8 + (g - 1))
                elif not first:
                    pe.wait_ge(op_done, b * 64 + (g - 1))
                if g < 4:
                    pe.wait_ge(xn_ready, b * 4 + (g + 1))
                    for k in range(KD):
                        mm = nc.tensor.transpose(turn_bank[g % 2][:, k, :], xn[g % 2][:, k * P:(k + 1) * P], ident[:])
                else:
                    if g == 4:
                        pe.wait_ge(kv_roped, b * 2 + 2)
                    for i, lt in enumerate(GROUPS[g - 4]):
                        mm = nc.tensor.transpose(turn_bank[g % 2][:, i, :], kv_r[:, lt, :], ident[:])
                mm.then_inc(pro_turned, 1)

            def batch(b, first, last):
                n0 = b * H
                for g in range(4):
                    turn_inputs(b, first, g)
                pe.wait_ge(pro_lo, b * 8 + 4)
                chain_a(n0)
                if first:
                    fold_score(0, ctx_bank)
                turn_inputs(b, first, 4)
                for m in range(QT):
                    chain_b(n0, m)
                    turn_inputs(b, first, m + 5)
                chain_c(n0)
                if first:
                    pe.wait_ge(copied_g, 1)
                    fold_score(1, ctx_bank)
                pe.wait_ge(pro_lo, b * 8 + 8)
                heads_of(pe, b, head, first, last)

            pe.wait_ge(ident_ready, 1)
            batches(pe, batch)

        @block.scalar
        def _(act):
            def hi(out, in_):
                return nc.scalar.activation(out, in_, ACT.Copy)

            def chain_hi(n, m):
                act.wait_ge(rope_sum, n * 3 + (m + 1))
                hi(qr[0][:, m, :], straight[:, m, :]).then_inc(rope_hi, 1)

            def turn_hi(n, h, t, g):
                act.wait_ge(e_turned, n * 16 + (4 * t + g + 1))
                half, k = t // 2, len(GROUPS[g])
                rows = P if g < 3 else LR
                if g == 0 and t % 2 == 0 and h != 0:
                    act.wait_ge(pv_done, n * 2 + (half - 1))
                hi(eT[half][0][0:rows, 4 * g:4 * g + k, (t % 2) * P:(t % 2 + 1) * P], turn_bank[g % 2][0:rows, 0:k, :]).then_inc(e_hi, 1)

            def query_weights_hi(n, first=False):
                act.wait_ge(wq_loaded, n * 16 + 16)
                if not first:
                    act.wait_ge(qa_ready, n)
                hi(wq[0][:], wq_in[:]).then_inc(wq_hi, 1)

            def rotary_weights_hi(n, fold, first=False):
                if fold:
                    act.wait_ge(wr_loaded, n * 16 + 16)
                    act.wait_ge(copied_g, n + 1)
                else:
                    act.wait_ge(wr_loaded, n * 32 - (16 * H - 32))
                if not first:
                    act.wait_ge(qc_ready, n)
                hi(wr[0][:], wr_in[:]).then_inc(wr_hi, 1)

            def context_hi(n, half):
                act.wait_ge(pv_done, n * 2 + (half + 1))
                cols = slice(half * HW, (half + 1) * HW)
                hi(ctxT[0][:, cols], ctx_bank[:, cols]).then_inc(ctx_hi, 1)

            def head(at):
                n = at.n
                for t in range(ST):
                    if t == 2 and at.has(-1):
                        context_hi(n - 1, 1)
                    for g in range(4):
                        if t > 0 and at.has(0):
                            turn_hi(n, at.h, t - 1, g)
                        if t == 0 and at.has(-1):
                            turn_hi(n - 1, None, ST - 1, g)
                        if t == 3 and g == 1 and at.has(1):
                            chain_hi(n + 1, 2)
                        if t == 0 and g == 1 and at.has(1):
                            rotary_weights_hi(n + 1, at.fold)
                    if t == 2 and at.has(1):
                        chain_hi(n + 1, 0)
                        chain_hi(n + 1, 1)
                    if t == 0 and at.has(-1):
                        context_hi(n - 1, 0)
                    if t == 0 and at.h == H and at.next_batch is not None:
                        norm_root(at.next_batch)
                    if t == 3 and at.has(1):
                        act.wait_ge(qc_ready, n + 2)
                        hi(qc[1 - at.p][0][:], item_bank[:]).then_inc(qc_hi, 1)
                    if at.has(0):
                        act.wait_ge(nmax_ready, n * 4 + (t + 1))
                        for c, (lo, _, width) in enumerate(CHUNKS):
                            nc.scalar.activation(e32[t % 2][:, lo:lo + width], score_bank[:, c, 0:width], ACT.Exp,
                                                 bias=nmax[:, at.p, t:t + 1],
                                                 accum_out=sums[:, at.p, t, c:c + 1]).then_inc(exp_done, 1)
                    if t == 0 and at.has(1):
                        act.wait_ge(qa_ready, n + 2)
                        hi(qk[0][:], item_bank[:]).then_inc(qa_hi, 1)
                    if t == 1 and at.has(-1):
                        if at.fold:
                            act.wait_ge(copied_o, n)
                        else:
                            act.wait_ge(wo_loaded, n * 16 - 16 * H)
                        if at.has(-2):
                            act.wait_ge(op_ready, n * 4 - 4)
                        hi(wo[0][:], wo_in[:]).then_inc(wo_hi, 1)
                    if t == 1 and at.has(2):
                        query_weights_hi(n + 2)

            def norm_root(b):
                act.wait_ge(eps_added, b + 1)
                nc.scalar.activation(std[:], var[:], ACT.Sqrt).then_inc(std_ready, 1)

            def inputs_hi(b, g):
                act.wait_ge(pro_turned, b * 8 + (g + 1))
                if g < 4:
                    hi(xnT[0][:, :, g * P:(g + 1) * P], turn_bank[g % 2][:]).then_inc(pro_hi, 1)
                else:
                    k = len(GROUPS[g - 4])
                    lo = GROUPS[g - 4][0] * P
                    hi(kvT[0][:, lo:lo + k * P], turn_bank[g % 2][:, 0:k, :].rearrange("p k c -> p (k c)")).then_inc(pro_hi, 1)

            def batch(b, first, last):
                n0 = b * H
                query_weights_hi(n0, first)
                if not first:
                    rotary_weights_hi(n0, False)
                if not first:
                    act.wait_ge(op_done, n0 * 4)
                    act.dma_start(x1_dram[:, bass.ds(b * ST - ST, ST), :], x1[:]).then_inc(x1_stored, 16)
                act.wait_ge(kv_mult, b * 3 + 3)
                for g in range(4):
                    inputs_hi(b, g)
                act.wait_ge(qa_ready, n0 + 1)
                hi(qk[0][:], item_bank[:]).then_inc(qa_hi, 1)
                if first:
                    rotary_weights_hi(n0, True, True)
                query_weights_hi(n0 + 1)
                inputs_hi(b, 4)
                inputs_hi(b, 5)
                inputs_hi(b, 6)
                chain_hi(n0, 0)
                chain_hi(n0, 1)
                inputs_hi(b, 7)
                chain_hi(n0, 2)
                hi(kvl[0][:], kv_r[:]).then_inc(kv_hi, 1)
                act.wait_ge(qc_ready, n0 + 1)
                hi(qc[0][0][:], item_bank[:]).then_inc(qc_hi, 1)
                act.wait_ge(kv_lo, b + 1)
                heads_of(act, b, head, first, last)

            norm_root(0)
            batches(act, batch)
            act.wait_ge(op_done, B * H * 4)
            act.dma_start(x1_dram[:, B * ST - ST:B * ST, :], x1[:]).then_inc(x1_stored, 16)

        @block.vector
        def _(dve):
            def low(out, full, high):
                return nc.vector.tensor_tensor(out, full, f32(high), ALU.subtract)

            def chain_rope(n, m, first=False):
                dve.wait_ge(qb_ready, n * 3 + (m + 1))
                if m == 0 and not first:
                    dve.wait_ge(rope_lo, n * 3)
                nc.vector.tensor_tensor(straight[:, m, :], item_bank[:], cos_q[:, m, :], ALU.mult)
                if m < 2:
                    nc.vector.tensor_tensor(turned_q[:, 1 - m, :], item_bank[:], sin_q[:, m, :], ALU.mult).then_inc(rope_mult, 1)
                else:
                    nc.vector.tensor_tensor(turned_q[64:P, m, :], item_bank[0:64, :], sin_q[0:64, m, :], ALU.mult)
                    nc.vector.tensor_tensor(turned_q[0:64, m, :], item_bank[64:P, :], sin_q[64:P, m, :], ALU.mult).then_inc(rope_mult, 1)

            def turn_lo(n, t, g):
                dve.wait_ge(e_hi, n * 16 + (4 * t + g + 1))
                half, k = t // 2, len(GROUPS[g])
                rows = P if g < 3 else LR
                cols = slice((t % 2) * P, (t % 2 + 1) * P)
                low(eT[half][1][0:rows, 4 * g:4 * g + k, cols], turn_bank[g % 2][0:rows, 0:k, :],
                    eT[half][0][0:rows, 4 * g:4 * g + k, cols]).then_inc(e_lo, 1)

            def reciprocal(n, p):
                dve.wait_ge(exp_done, n * 16 + 16)
                nc.vector.tensor_reduce(rsum[:], sums[:, p], AX.X, ALU.add).then_inc(sum_done, 1)
                dve.wait_ge(sum_done, n + 1)
                nc.vector.reciprocal(recip[:, p], rsum[:]).then_inc(recip_done, 1)

            def copy_g(n, bank):
                dve.wait_ge(made_g, n + 1)
                if not (isinstance(n, int) and n == 0):
                    dve.wait_ge(wr_lo, n)
                    dve.wait_ge(g_stored, n * 16)
                nc.vector.tensor_copy(wr_in[:, CQ:2 * CQ], bank[:, 0:CQ]).then_inc(copied_g, 1)

            def copy_o(n):
                dve.wait_ge(made_o, n + 1)
                if not (isinstance(n, int) and n == 0):
                    dve.wait_ge(wo_lo, n)
                    dve.wait_ge(o_stored, n * 16)
                nc.vector.tensor_copy(wo_in[:], turn_bank[1][:].rearrange("p k c -> p (k c)")).then_inc(copied_o, 1)

            def context_lo(n, half):
                dve.wait_ge(ctx_hi, n * 2 + (half + 1))
                cols = slice(half * HW, (half + 1) * HW)
                low(ctxT[1][:, cols], ctx_bank[:, cols], ctxT[0][:, cols]).then_inc(ctx_lo, 1)

            def add_output(n, p, j, first):
                dve.wait_ge(op_ready, n * 4 + (j + 1))
                if j == 0:
                    dve.wait_ge(recip_done, n + 1)
                if not first:
                    dve.wait_ge(op_done, n * 4 + (j - 3))
                out = turn_bank[j % 2][:].rearrange("p k c -> p (k c)")
                so_far = x_next if first else x1
                nc.vector.scalar_tensor_tensor(x1[:, j, :], out, recip[:, p, j:j + 1], so_far[:, j, :],
                                               ALU.mult, ALU.add).then_inc(op_done, 1)

            def norm_stats(b):
                dve.wait_ge(x_in, b * 16 + 16)
                for t in range(ST):
                    nc.vector.bn_stats(stats[:, t, :], x_next[:, t, :]).then_inc(stat_made, 1)
                dve.wait_ge(stat_made, b * 4 + 4)
                nc.vector.memset(rsum[:], 0.0)
                for t in range(ST):
                    nc.vector.bn_aggr(mv[:, t, :], stats[:, t, :]).then_inc(var_ready, 1)
                dve.wait_ge(var_ready, b * 4 + 4)
                nc.vector.tensor_scalar(var[:], mv[:, :, 1], LN_EPS, None, ALU.add).then_inc(eps_added, 1)

            def norm(b, t):
                if t == 0:
                    dve.wait_ge(std_ready, b + 1)
                    nc.vector.reciprocal(rstd[:], std[:]).then_inc(rstd_ready, 1)
                    dve.wait_ge(rstd_ready, b + 1)
                if t >= 2:
                    dve.wait_ge(pro_turned, b * 8 + (t - 1))
                nc.vector.tensor_scalar(xn[t % 2][:], x_next[:, t, :], mv[:, t, 0:1], rstd[:, t:t + 1],
                                        ALU.subtract, ALU.mult).then_inc(xn_ready, 1)

            two = lambda ap: ap.rearrange("p t (f two) -> p t f two", two=2)
            hc, fc = C // 2, C // 4

            def trig(which, lo, hi):
                return trig_k[:, which, :, lo:hi].rearrange("p t (f o) -> p t f o", o=1).broadcast_to([P, LT, hi - lo, 2])

            def rope_keys_products(b, first):
                dve.wait_ge(kv_loaded, b * 32 + 32)
                if not first:
                    dve.wait_ge(pv_done, b * 2 * H - 1)
                nc.vector.tensor_tensor(two(kv_t[:, :, 0:hc]), two(kv_in[:, :, hc:C]), trig(1, 0, fc), ALU.mult).then_inc(kv_mult, 1)
                nc.vector.tensor_tensor(two(kv_t[:, :, hc:C]), two(kv_in[:, :, 0:hc]), trig(1, fc, hc), ALU.mult).then_inc(kv_mult, 1)
                nc.vector.tensor_tensor(two(kv_r[:]), two(kv_in[:]), trig(0, 0, hc), ALU.mult).then_inc(kv_mult, 1)

            def rope_keys_sums(b):
                dve.wait_ge(kv_mult, b * 3 + 3)
                nc.vector.tensor_tensor(kv_r[:, :, 0:hc], kv_r[:, :, 0:hc], kv_t[:, :, 0:hc], ALU.subtract).then_inc(kv_roped, 1)
                nc.vector.tensor_tensor(kv_r[:, :, hc:C], kv_r[:, :, hc:C], kv_t[:, :, hc:C], ALU.add).then_inc(kv_roped, 1)

            def head(at):
                n = at.n
                for t in range(ST):
                    if t == 2 and at.has(-1):
                        context_lo(n - 1, 1)
                    for c, (_, _, width) in enumerate(CHUNKS):
                        if at.has(0):
                            dve.wait_ge(scores_ready, n * 16 + (4 * t + c + 1))
                            nc.vector.tensor_reduce(mx[:, c:c + 1], score_bank[:, c, 0:width], AX.X, ALU.max).then_inc(max_part, 1)
                        if t > 0 and at.has(0):
                            turn_lo(n, t - 1, c)
                        if t == 0 and at.has(-1):
                            turn_lo(n - 1, ST - 1, c)
                    if at.has(0):
                        dve.wait_ge(max_part, n * 16 + (4 * t + 4))
                        nc.vector.tensor_reduce(nmax[:, at.p, t:t + 1], mx[:], AX.X, ALU.max, negate=True).then_inc(nmax_ready, 1)
                    if t == 1 and at.has(-1):
                        reciprocal(n - 1, 1 - at.p)
                    if t == 0:
                        if at.has(-1):
                            context_lo(n - 1, 0)
                            if at.fold:
                                copy_o(n - 1)
                        if at.has(1):
                            dve.wait_ge(qa_hi, n + 2)
                            low(qk[1][:], item_bank[:], qk[0][:]).then_inc(qa_lo, 1)
                    if t == 1:
                        if at.has(1):
                            chain_rope(n + 1, 0)
                        if at.has(2) and at.fold:
                            copy_g(n + 2, turn_bank[0][:].rearrange("p k c -> p (k c)"))
                        if at.has(1):
                            chain_rope(n + 1, 1)
                    if t == 2:
                        if at.has(1):
                            chain_rope(n + 1, 2)
                        if at.has(-1):
                            if at.h == 1 and at.stored is not None:
                                dve.wait_ge(x1_stored, at.stored * 16)
                            add_output(n - 1, 1 - at.p, 0, at.h == 1)
                            add_output(n - 1, 1 - at.p, 1, at.h == 1)
                    if t == 0 and at.h == H and at.next_batch is not None:
                        norm(at.next_batch, 0)
                        norm(at.next_batch, 1)
                        rope_keys_products(at.next_batch, False)
                    if t == 3:
                        if at.has(1):
                            dve.wait_ge(qc_hi, n + 2)
                            low(qc[1 - at.p][1][:], item_bank[:], qc[1 - at.p][0][:]).then_inc(qc_lo, 1)
                        if at.has(-1):
                            add_output(n - 1, 1 - at.p, 2, at.h == 1)
                            add_output(n - 1, 1 - at.p, 3, at.h == 1)
                    if t == 0 and at.h == H - 1 and at.next_batch is not None:
                        dve.wait_ge(qa_ready, n + 1)
                        pad_keys()
                    if t == 3 and at.h == H - 1 and at.next_batch is not None:
                        norm_stats(at.next_batch)

            def pad_keys():
                nc.vector.tensor_tensor(kv_in[:, LT - 1, :], ident[:], ident[:], ALU.subtract).then_inc(pad_ready, 1)

            def inputs_low(b, g):
                dve.wait_ge(pro_hi, b * 8 + (g + 1))
                if g < 4:
                    low(xnT[1][:, :, g * P:(g + 1) * P], turn_bank[g % 2][:], xnT[0][:, :, g * P:(g + 1) * P]).then_inc(pro_lo, 1)
                else:
                    k = len(GROUPS[g - 4])
                    lo = GROUPS[g - 4][0] * P
                    low(kvT[1][:, lo:lo + k * P], turn_bank[g % 2][:, 0:k, :].rearrange("p k c -> p (k c)"),
                        kvT[0][:, lo:lo + k * P]).then_inc(pro_lo, 1)

            def first_rope(n, m):
                dve.wait_ge(rope_mult, n * 3 + max(2, m + 1))
                nc.vector.tensor_tensor(straight[:, m, :], straight[:, m, :], turned_q[:, m, :], ALU.add).then_inc(rope_sum, 1)

            def batch(b, first, last):
                n0 = b * H
                for g in range(4):
                    inputs_low(b, g)
                    if g < 2:
                        norm(b, g + 2)
                rope_keys_sums(b)
                if first:
                    dve.wait_ge(tables_in, 32)
                dve.wait_ge(qa_hi, n0 + 1)
                low(qk[1][:], item_bank[:], qk[0][:]).then_inc(qa_lo, 1)
                if first:
                    copy_g(0, ctx_bank)
                inputs_low(b, 4)
                chain_rope(n0, 0, True)
                inputs_low(b, 5)
                chain_rope(n0, 1, True)
                first_rope(n0, 0)
                first_rope(n0, 1)
                inputs_low(b, 6)
                chain_rope(n0, 2, True)
                first_rope(n0, 2)
                inputs_low(b, 7)
                dve.wait_ge(rope_hi, n0 * 3 + 3)
                dve.wait_ge(rope_lo, n0 * 3 + 2)
                low(qr[1][:, 2, :], straight[:, 2, :], qr[0][:, 2, :]).then_inc(rope_lo, 1)
                dve.wait_ge(qc_hi, n0 + 1)
                low(qc[0][1][:], item_bank[:], qc[0][0][:]).then_inc(qc_lo, 1)
                if first:
                    copy_g(1, ctx_bank)
                dve.wait_ge(kv_hi, b + 1)
                low(kvl[1][:], kv_r[:], kvl[0][:]).then_inc(kv_lo, 1)
                heads_of(dve, b, head, first, last)

            dve.wait_ge(ident_ready, 1)
            pad_keys()
            norm_stats(0)
            norm(0, 0)
            norm(0, 1)
            dve.wait_ge(rotary_in, 16)
            rope_keys_products(0, True)
            batches(dve, batch)

def experts(nc, mem, sem, x1_dram, x1_stored, early, ew_lo, experts_in, weights_in, proj_w, out):
    sb = lambda name, shape, dt=F32: mem.enter_context(nc.sbuf_tensor(name, shape, dt))
    pair = lambda name, shape: (sb(name + "_hi", shape, F32R), sb(name + "_lo", shape, F32R))
    ew = (sb("ew_hi", [P, E * KD, D], F32R), ew_lo)
    with ExitStack() as whole:
        pw_in = whole.enter_context(nc.sbuf_tensor("pw_in", [P, KD, D], F32))
    pw_lo = sb("pw_lo", [P, KD, D], F32R)
    pw = (sb("pw_hi", [P, KD, D], F32R), pw_lo)
    whole_weights = lambda e: pw_in[:] if e == E else early["ew"][:, e * KD:(e + 1) * KD, :]
    split_weights = lambda e: tuple(w[:] for w in pw) if e == E else tuple(w[:, e * KD:(e + 1) * KD, :] for w in ew)
    rw = sb("rw", [P, KD, 2, E], F32R)
    zT = [pair(f"zT{p}", [P, KD, P]) for p in (0, 1)]
    combT = pair("combT", [P, KD, P])
    eb, pb, nw, rb, rw_in, lane, x_norm = (early[name] for name in ("eb", "pb", "nw", "rb", "rw_in", "lane", "x_norm"))
    ident = sb("ident2", [P, P])
    x_res, z, y = sb("x_res", [P, D]), sb("z", [P, D]), sb("y", [P, D])
    hid = [sb(f"hid{i}", [P, D]) for i in (0, 1)]
    z_res = [sb(f"z_res{p}", [P, D]) for p in (0, 1)]
    comb = [sb(f"comb{p}", [P, D]) for p in (0, 1)]
    small = sb("small", [P, 64])
    col = lambda i, n=1: small[:, i:i + n]
    stats, mv, var, std, rstd = col(0, 6), col(6, 2), col(8), col(9), col(10)
    ss, ms, rms, rrms = col(11), col(12), col(13), col(14)
    diff, ratio, den, w1, w2, idxf = col(15), col(16), col(17), col(18), col(19), col(20, 2)
    logits, top, hot1, hot2 = col(24, 8), col(32, 8), col(40, 8), col(48, 8)
    idx = sb("idx", [P, 8], U32)
    full_w = [sb(f"full_w{p}", [P, E]) for p in (0, 1)]
    psum = lambda name, shape: mem.enter_context(nc.psum_tensor(name, shape, F32))
    hid_bank = [psum(f"hid_bank{i}", [P, D]) for i in range(4)]
    comb_bank, z_bank = psum("comb_bank", [P, KD, P]), psum("z_bank", [P, KD, P])
    proj_bank, router_bank = psum("proj_bank", [P, D]), psum("router_bank", [P, D])

    names = """pw_in w_hi w_lo rw_hi rw_lo xn_in res_in res_ready id_zero id_ready
        z_stat z_mv z_var z_std z_rstd z_ready z_turned z_hi z_lo routed route_step diff_ready ratio_ready
        weights_ready hid_ready hid_added act_done comb_step comb_turned comb_hi comb_lo projected
        y_ready squared ms_ready rms_ready rrms_ready fin_ready out_ready out_stored""".split()
    s = {name: sem("x_" + name) for name in names}
    EARLY_DMAS = 16 * (6 + E)
    f32 = lambda ap: ap.bitcast(F32)

    with nc.Block() as block:

        @block.sync
        def _(sp):
            sp.wait_ge(x1_stored, 16 * B)
            sp.dma_start(pw_in[:], proj_w).then_inc(s["pw_in"], 16)

            def load_norm(n):
                sp.wait_ge(s["z_ready"], n)
                sp.dma_start(x_norm[:], x1_dram[:, bass.ds(n, 1)].rearrange("p a d -> p (a d)")).then_inc(s["xn_in"], 16)

            load_norm(1)
            with sp.Fori(2, NT) as n:
                load_norm(n)

        @block.gpsimd
        def _(pool):
            nc.gpsimd.memset(ident[:], 0.0).then_inc(s["id_zero"], 1)
            pool.wait_ge(s["id_zero"], 1)
            nc.gpsimd.affine_select(out=ident[:], in_=ident[:], compare_op=ALU.not_equal, fill=1.0, base=0,
                                    pattern=[[-1, P]], channel_multiplier=1).then_inc(s["id_ready"], 1)
            pool.wait_ge(experts_in, EARLY_DMAS)
            out_rows = out.rearrange("b s d -> (b s) d").rearrange("(n p) d -> p n d", p=P)
            one = lambda v, n: v[:, bass.ds(n, 1)].rearrange("p a d -> p (a d)")

            def store(n):
                pool.wait_ge(s["fin_ready"], n + 1)
                pool.wait_ge(s["res_in"], n * 16 + 16)
                nc.gpsimd.tensor_tensor(y[:], y[:], x_res[:], ALU.add).then_inc(s["out_ready"], 1)
                pool.wait_ge(s["out_ready"], n + 1)
                pool.dma_start(one(out_rows, n), y[:]).then_inc(s["out_stored"], 16)

            pool.wait_ge(s["z_ready"], 1)
            nc.gpsimd.tensor_tensor(z_res[0][:], z[:], pb[:], ALU.add).then_inc(s["res_ready"], 1)
            pool.dma_start(x_res[:], x1_dram[:, 0, :]).then_inc(s["res_in"], 16)
            pool.wait_ge(s["z_ready"], 2)
            nc.gpsimd.tensor_tensor(z_res[1][:], z[:], pb[:], ALU.add).then_inc(s["res_ready"], 1)
            with pool.Fori(0, NT // 2 - 1) as i:
                for p in (0, 1):
                    n = i * 2 + p
                    store(n)
                    pool.dma_start(x_res[:], one(x1_dram, n + 1)).then_inc(s["res_in"], 16)
                    pool.wait_ge(s["z_ready"], n + 3)
                    nc.gpsimd.tensor_tensor(z_res[p][:], z[:], pb[:], ALU.add).then_inc(s["res_ready"], 1)
            store(NT - 2)
            pool.dma_start(x_res[:], x1_dram[:, NT - 1, :]).then_inc(s["res_in"], 16)
            store(NT - 1)
            pool.wait_ge(s["out_stored"], 16 * NT)

        @block.tensor
        def _(pe):
            def split_product(out_ap, w, xx, first, last):
                nc.tensor.matmul(out_ap, w[0], xx[0], start=first, stop=False)
                nc.tensor.matmul(out_ap, w[0], xx[1], start=False, stop=False)
                return nc.tensor.matmul(out_ap, w[1], xx[0], start=False, stop=last)

            def turn(bank, src, done):
                for k in range(KD):
                    mm = nc.tensor.transpose(bank[:, k, :], src[:, k * P:(k + 1) * P], ident[:])
                mm.then_inc(done, 1)

            def over_width(bank, w, x_of, done):
                for k in range(KD):
                    mm = split_product(bank, [t[:, k, :] for t in w], x_of(k), k == 0, k == KD - 1)
                mm.then_inc(done, 1)

            def turn_z(n):
                pe.wait_ge(s["z_ready"], n + 1)
                turn(z_bank, z, s["z_turned"])

            def route(n, p):
                pe.wait_ge(s["z_lo"], n + 1)
                for k in range(KD):
                    nc.tensor.matmul(router_bank[:, 0:2 * E], zT[p][0][:, k, :], rw[:, k].rearrange("p a e -> p (a e)"),
                                     start=k == 0, stop=False)
                    mm = nc.tensor.matmul(router_bank[:, 0:E], zT[p][1][:, k, :], rw[:, k, 0, :],
                                          start=False, stop=k == KD - 1)
                mm.then_inc(s["routed"], 1)

            def tile(at):
                n, p = at.n, at.p
                for e in range(E):
                    if at.has(0):
                        if at.h == 0:
                            pe.wait_ge(s["w_lo"], e + 1)
                        if at.h != 0 or e >= 4:
                            pe.wait_ge(s["hid_added"], n * E + (e - 3))
                        over_width(hid_bank[e % 4][:], zT[p], lambda k: [t[:, e * KD + k, :] for t in ew], s["hid_ready"])
                    if e == 2 and at.has(-1):
                        pe.wait_ge(s["comb_step"], n * E)
                        turn(comb_bank, comb[1 - p], s["comb_turned"])
                    if e == 3 and at.has(1):
                        turn_z(n + 1)
                    if e == 4 and at.has(-1):
                        if at.h == 1:
                            pe.wait_ge(s["w_lo"], E + 1)
                        pe.wait_ge(s["comb_lo"], n)
                        over_width(proj_bank[:], combT, lambda k: [t[:, k, :] for t in pw], s["projected"])
                    if e == 5 and at.has(1):
                        route(n + 1, 1 - p)

            pe.wait_ge(s["id_ready"], 1)
            turn_z(0)
            pe.wait_ge(s["rw_lo"], 1)
            route(0, 0)
            heads_of(pe, 0, tile)

        @block.scalar
        def _(act):
            def hi(out_ap, in_):
                return nc.scalar.activation(out_ap, in_, ACT.Copy)

            def z_root(n):
                act.wait_ge(s["z_var"], n + 1)
                nc.scalar.activation(std, var, ACT.Sqrt).then_inc(s["z_std"], 1)

            def z_high(n, p):
                act.wait_ge(s["z_turned"], n + 1)
                hi(zT[p][0][:], z_bank[:]).then_inc(s["z_hi"], 1)

            def ratio_of(n):
                act.wait_ge(s["diff_ready"], n + 1)
                nc.scalar.activation(ratio, diff, ACT.Exp).then_inc(s["ratio_ready"], 1)

            def tile(at):
                n, p = at.n, at.p
                for e in range(E):
                    if at.has(0):
                        act.wait_ge(s["hid_added"], n * E + (e + 1))
                        nc.scalar.activation(hid[e % 2][:], hid[e % 2][:], ACT.Silu).then_inc(s["act_done"], 1)
                        if at.h == 0 and e + 3 <= E:
                            weights_high(e + 3)
                        if at.h == 0 and e == 1:
                            z_root(1)
                    if e == 2 and at.has(-1):
                        act.wait_ge(s["comb_turned"], n)
                        hi(combT[0][:], comb_bank[:]).then_inc(s["comb_hi"], 1)
                    if e == 4 and at.has(1):
                        z_high(n + 1, 1 - p)
                    if e == 5 and at.has(-1):
                        act.wait_ge(s["y_ready"], n)
                        nc.scalar.activation(proj_bank[:], y[:], ACT.Square, accum_out=ss).then_inc(s["squared"], 1)
                    if e == 6 and at.has(1):
                        ratio_of(n + 1)
                    if e == 6 and at.has(-1):
                        act.wait_ge(s["ms_ready"], n)
                        nc.scalar.activation(rms, ms, ACT.Sqrt).then_inc(s["rms_ready"], 1)
                    if e == 6 and at.has(2):
                        z_root(n + 2)

            def weights_high(e):
                act.wait_ge(s["pw_in"] if e == E else weights_in[e], 16)
                hi(split_weights(e)[0], whole_weights(e)).then_inc(s["w_hi"], 1)

            act.wait_ge(experts_in, EARLY_DMAS)
            hi(rw[:, :, 0, :], rw_in[:]).then_inc(s["rw_hi"], 1)
            z_root(0)
            z_high(0, 0)
            weights_high(0)
            ratio_of(0)
            weights_high(1)
            weights_high(2)
            heads_of(act, 0, tile)

        @block.vector
        def _(dve):
            def low(out_ap, full, high):
                return nc.vector.tensor_tensor(out_ap, full, f32(high), ALU.subtract)

            def z_stats(n):
                if not (isinstance(n, int) and n == 0):
                    dve.wait_ge(s["xn_in"], n * 16)
                nc.vector.bn_stats(stats, x_norm[:]).then_inc(s["z_stat"], 1)
                dve.wait_ge(s["z_stat"], n + 1)
                nc.vector.memset(col(56), 0.0)
                nc.vector.bn_aggr(mv, stats).then_inc(s["z_mv"], 1)
                dve.wait_ge(s["z_mv"], n + 1)
                nc.vector.tensor_scalar(var, small[:, 7:8], LN_EPS, None, ALU.add).then_inc(s["z_var"], 1)

            def z_norm(n):
                dve.wait_ge(s["z_std"], n + 1)
                nc.vector.reciprocal(rstd, std).then_inc(s["z_rstd"], 1)
                dve.wait_ge(s["z_rstd"], n + 1)
                dve.wait_ge(s["z_turned"], n)
                dve.wait_ge(s["res_ready"], n)
                nc.vector.tensor_scalar(z[:], x_norm[:], small[:, 6:7], rstd, ALU.subtract, ALU.mult).then_inc(s["z_ready"], 1)

            def z_low(n, p):
                dve.wait_ge(s["z_hi"], n + 1)
                low(zT[p][1][:], z_bank[:], zT[p][0][:]).then_inc(s["z_lo"], 1)

            def pick(n):
                def step(i, ins):
                    ins.then_inc(s["route_step"], 1)
                    dve.wait_ge(s["route_step"], n * 10 + (i + 1))
                dve.wait_ge(s["routed"], n + 1)
                step(0, nc.vector.tensor_tensor(logits, router_bank[:, E:2 * E], rb[:], ALU.add))
                step(1, nc.vector.tensor_tensor(logits, router_bank[:, 0:E], logits, ALU.add))
                nc.vector.memset(col(57), 0.0)
                step(2, nc.vector.max(top, logits))
                nc.vector.tensor_tensor(diff, small[:, 33:34], small[:, 32:33], ALU.subtract).then_inc(s["diff_ready"], 1)
                step(3, nc.vector.max_index(idx[:], top, logits))
                step(4, nc.vector.tensor_copy(idxf, idx[:, 0:2]))
                nc.vector.tensor_scalar(hot1, lane[:], small[:, 20:21], None, ALU.is_equal)
                step(5, nc.vector.tensor_scalar(hot2, lane[:], small[:, 21:22], None, ALU.is_equal))

            def weigh(n, p):
                def step(i, ins):
                    ins.then_inc(s["route_step"], 1)
                    dve.wait_ge(s["route_step"], n * 10 + (i + 1))
                dve.wait_ge(s["ratio_ready"], n + 1)
                step(6, nc.vector.tensor_scalar(den, ratio, 1.0, None, ALU.add))
                step(7, nc.vector.reciprocal(w1, den))
                step(8, nc.vector.tensor_tensor(w2, ratio, w1, ALU.mult))
                step(9, nc.vector.tensor_scalar(hot1, hot1, w1, None, ALU.mult))
                nc.vector.scalar_tensor_tensor(full_w[p][:], hot2, w2, hot1, ALU.mult, ALU.add).then_inc(s["weights_ready"], 1)

            def combine(at, e):
                n, p = at.n, at.p
                dve.wait_ge(s["act_done"], n * E + (e + 1))
                w = full_w[p][:, e:e + 1]
                if e == 0:
                    dve.wait_ge(s["weights_ready"], n + 1)
                    nc.vector.tensor_scalar(comb[p][:], hid[0][:], w, None, ALU.mult).then_inc(s["comb_step"], 1)
                else:
                    dve.wait_ge(s["comb_step"], n * E + e)
                    nc.vector.scalar_tensor_tensor(comb[p][:], hid[e % 2][:], w, comb[p][:], ALU.mult, ALU.add).then_inc(s["comb_step"], 1)

            def tile(at):
                n, p = at.n, at.p
                for e in range(E):
                    if at.has(0):
                        dve.wait_ge(s["hid_ready"], n * E + (e + 1))
                        if at.h != 0 or e >= 2:
                            dve.wait_ge(s["comb_step"], n * E + (e - 1))
                        nc.vector.tensor_tensor(hid[e % 2][:], hid_bank[e % 4][:], eb[:, e, :], ALU.add).then_inc(s["hid_added"], 1)
                        if e >= 1:
                            combine(at, e - 1)
                        if at.h == 0 and e + 2 <= E:
                            weights_low(e + 2)
                        if at.h == 0 and e == 1:
                            z_stats(1)
                    if e == 2 and at.has(1):
                        z_norm(n + 1)
                    if e == 2 and at.has(-1):
                        dve.wait_ge(s["comb_hi"], n)
                        low(combT[1][:], comb_bank[:], combT[0][:]).then_inc(s["comb_lo"], 1)
                    if e == 4 and at.has(1):
                        z_low(n + 1, 1 - p)
                    if e == 5 and at.has(-1):
                        dve.wait_ge(s["projected"], n)
                        dve.wait_ge(s["res_ready"], n)
                        if at.has(-2):
                            dve.wait_ge(s["out_stored"], n * 16 - 16)
                        nc.vector.tensor_tensor(y[:], proj_bank[:], z_res[1 - p][:], ALU.add).then_inc(s["y_ready"], 1)
                    if e == 6 and at.has(-1):
                        dve.wait_ge(s["squared"], n)
                        nc.vector.tensor_scalar(ms, ss, 1.0 / D, RMS_EPS, ALU.mult, ALU.add).then_inc(s["ms_ready"], 1)
                    if e == 5 and at.has(2):
                        z_stats(n + 2)
                    if e == 6 and at.has(1):
                        pick(n + 1)
                    if e == 7 and at.has(1):
                        weigh(n + 1, 1 - p)
                    if e == 7 and at.has(-1):
                        dve.wait_ge(s["rms_ready"], n)
                        nc.vector.reciprocal(rrms, rms).then_inc(s["rrms_ready"], 1)
                        dve.wait_ge(s["rrms_ready"], n)
                        nc.vector.scalar_tensor_tensor(y[:], y[:], rrms, nw[:], ALU.mult, ALU.mult).then_inc(s["fin_ready"], 1)
                if at.has(0):
                    combine(at, E - 1)

            def weights_low(e):
                dve.wait_ge(s["w_hi"], e + 1)
                low(split_weights(e)[1], whole_weights(e), split_weights(e)[0]).then_inc(s["w_lo"], 1)

            dve.wait_ge(s["rw_hi"], 1)
            low(rw[:, :, 1, :], rw_in[:], rw[:, :, 0, :]).then_inc(s["rw_lo"], 1)
            z_stats(0)
            z_norm(0)
            z_low(0, 0)
            weights_low(0)
            pick(0)
            weigh(0, 0)
            weights_low(1)
            heads_of(dve, 0, tile)



def _rope(length, dim):
    inv = np.float32(1.0) / np.float32(10000.0) ** (np.arange(0, dim, 2, dtype=np.float32) / np.float32(dim))
    f = np.arange(length, dtype=np.float32)[:, None] * inv[None, :].astype(np.float32)
    return np.repeat(np.sin(f), 2, axis=-1), np.repeat(np.cos(f), 2, axis=-1)


def _layout(inputs):
    a = {k: np.asarray(v) for k, v in inputs.items()}
    order = np.r_[0:128, 192:320, 128:192, 320:384]
    wq = a["L0_xattn_Wq"].reshape(H, K, KD, P).transpose(0, 3, 2, 1).reshape(H, P, D)
    w_first = np.concatenate([wq, a["L0_xattn_w_kc_q"][:, :, order]], axis=2)
    wo = a["L0_xattn_Wo"].reshape(D, H, K).transpose(1, 2, 0)
    w_fold = np.concatenate([a["L0_xattn_w_kc_kv"], wo], axis=2)
    w_score = np.concatenate([a["L0_xattn_W_qr"][:, order, :].transpose(0, 2, 1),
                              a["L0_xattn_W_kr"].transpose(0, 2, 1)], axis=2)
    sin, cos = _rope(S, CQ)
    pack = lambda t: t.T.reshape(QT, P, S).transpose(1, 0, 2)
    partner = np.r_[192:320, 0:128, 320:384, 128:192]
    sign = np.r_[np.ones(128), -np.ones(128), np.ones(64), -np.ones(64)].astype(np.float32)
    rope_q = np.stack([pack(cos[:, order]), pack(sin[:, partner] * sign)])
    sin, cos = _rope(L, C)
    pad = lambda t: np.concatenate([t, np.zeros((LT * P - L, C // 2), np.float32)]).reshape(LT, P, C // 2).transpose(1, 0, 2)
    rope_k = np.stack([pad(cos[:, ::2]), pad(sin[:, ::2])], axis=1)
    ew = a["L0_ffn_expert_w"].reshape(E, KD, P, D).transpose(0, 2, 1, 3)
    pw = a["L0_ffn_proj_w"].reshape(KD, P, D).transpose(1, 0, 2)
    rw = a["L0_ffn_router_w"].reshape(KD, P, E).transpose(1, 0, 2)
    iota = np.broadcast_to(np.arange(E, dtype=np.float32), (P, E))
    return {"x": a["x"], "kv": a["ctx_512"], "w_first": w_first, "w_fold": w_fold, "w_score": w_score,
            "router_w": rw, "router_b": a["L0_ffn_router_b"], "expert_w": ew, "expert_b": a["L0_ffn_expert_b"],
            "proj_w": pw, "proj_b": a["L0_ffn_proj_b"], "norm_w": a["L0_ffn_norm_w"],
            "rope_q": rope_q.astype(np.float32), "rope_k": rope_k.astype(np.float32), "iota": iota}


def kernel(**inputs):
    import concourse.bacc as _bacc
    from concourse.bass_utils import run_bass_kernel_spmd as _run

    nc = _bacc.Bacc("TRN2", target_bir_lowering=False, num_devices=1)
    arrays = {f"in_{k}": np.ascontiguousarray(v) for k, v in _layout(inputs).items()}
    args = [nc.dram_tensor(k, v.shape, mybir.dt.from_np(v.dtype), kind="ExternalInput").ap()
            for k, v in arrays.items()]
    args.append(nc.dram_tensor("out_dram", (B, S, D), F32, kind="ExternalOutput").ap())
    build(nc, *args)
    return _run(nc, [arrays], core_ids=[0]).results[0]["out_dram"]
```
